# Optimizing a Trainium2 kernel written in Bass

```python
import numpy as np
import jax
import jax.numpy as jnp

def _softmax(x, axis=-1):
    return jax.nn.softmax(x, axis=axis)

def _gelu(x):
    return jax.nn.gelu(x, approximate=True)

def _silu(x):
    return jax.nn.silu(x)

def _sigmoid(x):
    return jax.nn.sigmoid(x)

def _layernorm(x, axis=-1, eps=1e-05):
    m = jnp.mean(x, axis=axis, keepdims=True)
    v = jnp.var(x, axis=axis, keepdims=True)
    return (x - m) / jnp.sqrt(v + eps)

def _scatter_add(tgt, idx, src, axis=0):
    return tgt.at[idx].add(src)

def _segment_sum(src, seg, n):
    return jax.ops.segment_sum(src, seg, n)
kernel_name = 'mk_sandwich_d1_jaxref_r8_30c978'

def setup_inputs(seed: int=0):
    np.random.seed(seed)
    _w = jnp.asarray

    def _L0_attn_setup():
        import jax, jax.numpy as jnp
        from jax import lax
        import numpy as np
        D_MODEL, D_INNER, D_STATE, D_CONV, DT_RANK = (128, 256, 16, 4, 64)
        B, L = (2, 128)
        key = jax.random.key(seed)
        ks = jax.random.split(key, 10)
        s = lambda *sh: 1.0 / np.sqrt(sh[0])
        return {'x': jax.random.normal(ks[0], (B, L, D_MODEL), jnp.float32), 'W_in': jax.random.normal(ks[1], (D_MODEL, 2 * D_INNER), jnp.float32) * s(D_MODEL), 'conv_w': jax.random.normal(ks[2], (D_INNER, D_CONV), jnp.float32) * s(D_CONV), 'conv_b': jax.random.normal(ks[3], (D_INNER,), jnp.float32) * 0.1, 'W_x': jax.random.normal(ks[4], (D_INNER, DT_RANK + 2 * D_STATE), jnp.float32) * s(D_INNER), 'W_dt': jax.random.normal(ks[5], (DT_RANK, D_INNER), jnp.float32) * s(DT_RANK), 'b_dt': jax.random.uniform(ks[6], (D_INNER,), jnp.float32, -4.0, -2.0), 'A_log': jnp.log(jnp.broadcast_to(jnp.arange(1, D_STATE + 1, dtype=jnp.float32), (D_INNER, D_STATE))), 'D_param': jnp.ones((D_INNER,), jnp.float32), 'W_out': jax.random.normal(ks[7], (D_INNER, D_MODEL), jnp.float32) * s(D_INNER)}
    _L0_attn_in = _L0_attn_setup()

    def _L0_ffn_setup():
        import jax, jax.numpy as jnp
        import numpy as np
        D_MODEL = 128
        N_EXPERTS = 8
        TOP_K = 2
        D_FF = 256
        BATCH, SEQ = (2, 256)

        def _swiglu(x, w_gate, w_up, w_down):
            return jax.nn.silu(x @ w_gate.T) * (x @ w_up.T) @ w_down.T
        key = jax.random.key(seed)
        ks = jax.random.split(key, 10)
        sd = 1.0 / np.sqrt(D_MODEL)
        sf = 1.0 / np.sqrt(D_FF)
        return {'X': jax.random.normal(ks[0], (BATCH, SEQ, D_MODEL), dtype=jnp.float32), 'router_w': jax.random.normal(ks[1], (N_EXPERTS, D_MODEL), dtype=jnp.float32) * sd, 'expert_bias': jnp.zeros((N_EXPERTS,), dtype=jnp.float32), 'sw_gate': jax.random.normal(ks[2], (D_FF, D_MODEL), dtype=jnp.float32) * sd, 'sw_up': jax.random.normal(ks[3], (D_FF, D_MODEL), dtype=jnp.float32) * sd, 'sw_down': jax.random.normal(ks[4], (D_MODEL, D_FF), dtype=jnp.float32) * sf, 'ew_gate': jax.random.normal(ks[5], (N_EXPERTS, D_FF, D_MODEL), dtype=jnp.float32) * sd, 'ew_up': jax.random.normal(ks[6], (N_EXPERTS, D_FF, D_MODEL), dtype=jnp.float32) * sd, 'ew_down': jax.random.normal(ks[7], (N_EXPERTS, D_MODEL, D_FF), dtype=jnp.float32) * sf}
    _L0_ffn_in = _L0_ffn_setup()
    _d = {'L0_attn_x': _L0_attn_in['x'], 'L0_attn_W_in': _L0_attn_in['W_in'], 'L0_attn_conv_w': _L0_attn_in['conv_w'], 'L0_attn_conv_b': _L0_attn_in['conv_b'], 'L0_attn_W_x': _L0_attn_in['W_x'], 'L0_attn_W_dt': _L0_attn_in['W_dt'], 'L0_attn_b_dt': _L0_attn_in['b_dt'], 'L0_attn_A_log': _L0_attn_in['A_log'], 'L0_attn_D_param': _L0_attn_in['D_param'], 'L0_attn_W_out': _L0_attn_in['W_out'], 'L0_ffn_router_w': _L0_ffn_in['router_w'], 'L0_ffn_expert_bias': _L0_ffn_in['expert_bias'], 'L0_ffn_sw_gate': _L0_ffn_in['sw_gate'], 'L0_ffn_sw_up': _L0_ffn_in['sw_up'], 'L0_ffn_sw_down': _L0_ffn_in['sw_down'], 'L0_ffn_ew_gate': _L0_ffn_in['ew_gate'], 'L0_ffn_ew_up': _L0_ffn_in['ew_up'], 'L0_ffn_ew_down': _L0_ffn_in['ew_down']}
    _x0 = _d['L0_attn_x']
    _d['L0_attn_x'] = jax.random.normal(jax.random.fold_in(jax.random.key(seed), 1), (4, 512, 128), dtype=_x0.dtype)
    del _x0
    return _d

def reference(L0_attn_x, L0_attn_W_in, L0_attn_conv_w, L0_attn_conv_b, L0_attn_W_x, L0_attn_W_dt, L0_attn_b_dt, L0_attn_A_log, L0_attn_D_param, L0_attn_W_out, L0_ffn_router_w, L0_ffn_expert_bias, L0_ffn_sw_gate, L0_ffn_sw_up, L0_ffn_sw_down, L0_ffn_ew_gate, L0_ffn_ew_up, L0_ffn_ew_down):

    def _L0_attn_ref(x, W_in, conv_w, conv_b, W_x, W_dt, b_dt, A_log, D_param, W_out):
        import jax, jax.numpy as jnp
        from jax import lax
        import numpy as np
        D_MODEL, D_INNER, D_STATE, D_CONV, DT_RANK = (128, 256, 16, 4, 64)
        B, L = (2, 128)
        b, l, _ = x.shape
        d_inner, d_conv = conv_w.shape
        dt_rank = W_dt.shape[0]
        d_state = A_log.shape[1]
        xz = x @ W_in
        xs, z = jnp.split(xz, 2, axis=-1)
        xp = jnp.pad(xs, ((0, 0), (d_conv - 1, 0), (0, 0))).transpose(0, 2, 1)
        xc = lax.conv_general_dilated(xp, conv_w[:, None, :], (1,), 'VALID', feature_group_count=d_inner, dimension_numbers=('NCH', 'OIH', 'NCH'))
        xc = jax.nn.silu(xc.transpose(0, 2, 1) + conv_b)
        dbl = xc @ W_x
        dt = jax.nn.softplus(dbl[..., :dt_rank] @ W_dt + b_dt)
        Bm = dbl[..., dt_rank:dt_rank + d_state]
        Cm = dbl[..., dt_rank + d_state:]
        A = -jnp.exp(A_log)
        dA = jnp.exp(dt[..., None] * A)
        dBx = (dt * xc)[..., None] * Bm[:, :, None, :]

        def step(h, inp):
            dA_t, dBx_t, C_t = inp
            h = dA_t * h + dBx_t
            y = jnp.einsum('bdn,bn->bd', h, C_t)
            return (h, y)
        h0 = jnp.zeros((b, d_inner, d_state), x.dtype)
        _, ys = lax.scan(step, h0, (dA.transpose(1, 0, 2, 3), dBx.transpose(1, 0, 2, 3), Cm.transpose(1, 0, 2)))
        y = ys.transpose(1, 0, 2) + xc * D_param
        y = y * jax.nn.silu(z)
        return y @ W_out

    def _L0_ffn_ref(X, router_w, expert_bias, sw_gate, sw_up, sw_down, ew_gate, ew_up, ew_down):
        import jax, jax.numpy as jnp
        import numpy as np
        D_MODEL = 128
        N_EXPERTS = 8
        TOP_K = 2
        D_FF = 256
        BATCH, SEQ = (2, 256)

        def _swiglu(x, w_gate, w_up, w_down):
            return jax.nn.silu(x @ w_gate.T) * (x @ w_up.T) @ w_down.T
        B, S, D = X.shape
        x = X.reshape(-1, D)
        T = x.shape[0]
        logits = x @ router_w.T + expert_bias
        router_weights = jax.nn.softmax(logits, axis=-1)
        top_w, top_i = jax.lax.top_k(router_weights, TOP_K)
        top_w = jax.nn.softmax(top_w, axis=-1)
        shared = _swiglu(x, sw_gate, sw_up, sw_down)
        comb = jnp.zeros((T, N_EXPERTS), dtype=x.dtype)
        comb = comb.at[jnp.arange(T)[:, None], top_i].add(top_w)
        gate = jax.nn.silu(jnp.einsum('td,efd->etf', x, ew_gate))
        up = jnp.einsum('td,efd->etf', x, ew_up)
        expert_out = jnp.einsum('etf,edf->etd', gate * up, ew_down)
        specialist = jnp.einsum('te,etd->td', comb, expert_out)
        return (shared + specialist).reshape(B, S, D)
    x = L0_attn_x
    x = x + _layernorm(_L0_attn_ref(_layernorm(x, axis=-1), L0_attn_W_in, L0_attn_conv_w, L0_attn_conv_b, L0_attn_W_x, L0_attn_W_dt, L0_attn_b_dt, L0_attn_A_log, L0_attn_D_param, L0_attn_W_out), axis=-1)
    x = x + _layernorm(_L0_ffn_ref(_layernorm(x, axis=-1), L0_ffn_router_w, L0_ffn_expert_bias, L0_ffn_sw_gate, L0_ffn_sw_up, L0_ffn_sw_down, L0_ffn_ew_gate, L0_ffn_ew_up, L0_ffn_ew_down), axis=-1)
    return x

_drawn_inputs = setup_inputs


def setup_inputs(seed=0):
    import zlib

    import numpy as np

    out = dict(_drawn_inputs(seed))
    spreads = {'L0_attn_D_param': (1.0, 0.2), 'L0_ffn_expert_bias': (0.0, 0.1)}
    factors = {}
    for name, (base, spread) in spreads.items():
        noise = np.random.default_rng([zlib.crc32(name.encode()), seed]).standard_normal(out[name].shape)
        drawn = base * np.exp(spread * noise) if base else spread * noise
        out[name] = jnp.asarray(drawn.astype(out[name].dtype))
    for name, factor in factors.items():
        out[name] = (out[name] * factor).astype(out[name].dtype)
    return out
```

```python
from contextlib import ExitStack

import concourse.bass as bass
from concourse import mybir

F32 = mybir.dt.float32
ALU = mybir.AluOpType
ACT = mybir.ActivationFunctionType
AX_X = mybir.AxisListType.X

P = 128
SEQS, TOKENS, D_MODEL = 4, 512, 128
D_INNER, D_STATE, D_CONV, DT_RANK = 256, 16, 4, 64
HALVES = D_INNER // P
TILES = TOKENS // P
N_EXPERTS, D_FF = 8, 256
FFNS = N_EXPERTS + 1
PAD = D_CONV - 1
EPS = 1e-5

STEPS = SEQS * D_STATE
LEAD = 2
DA_RING = LEAD + 1
B_CHUNK = 4
B_CHUNKS = D_STATE // B_CHUNK
COMB_CHUNK = 2
COMB_RING = 4
UNITS = FFNS * 2

(PRE_STATS, PRE_NORM, PRE_CONV, PRE_GATE, PRE_DBL, PRE_DT, PRE_END) = range(7, 14)
(POST_TURN, POST_GATE, POST_STATS, POST_ADD, POST_NORM, ROUTE_A, ROUTE_B, ROUTE_C) = range(8)
UNIT_BASE, UNIT_SPAN = 7, 15
FIN_SLOT = UNIT_BASE + UNIT_SPAN
FIRST_SLOT = PRE_STATS - D_STATE
LAST_SLOT = STEPS + FIN_SLOT + 2


def pre_at(g, stage):
    s, r = divmod(g - stage + D_STATE, D_STATE)
    return s if r == 0 and 0 <= s < SEQS else None


def post_at(g, stage):
    s, r = divmod(g - stage, D_STATE)
    return s - 1 if r == 0 and 1 <= s <= SEQS else None


def units_at(g):
    return [(s, q) for s in range(SEQS) for q in range(UNITS)
            if D_STATE * (s + 1) + UNIT_BASE + q * UNIT_SPAN // UNITS == g]


def on_pool(q):
    return q % 2 == 0


def build(nc, x_in, cols, w_in, conv_t, w_x, w_dt, w_out, router_t, bias_r, gate_t, up_t, down_t,
          b_scratch, comb_scratch, out):
    with ExitStack() as ctx:
        def sb(name, shape, dt=F32):
            return ctx.enter_context(nc.sbuf_tensor(name, shape, dt))

        def bank(name):
            return ctx.enter_context(nc.psum_tensor(name, [P, TOKENS], F32))

        def sem(name):
            return ctx.enter_context(nc.semaphore(name))

        col_sb = sb("col_sb", [P, 3 * HALVES + HALVES * D_STATE])
        conv_b = col_sb[:, 0:2]
        b_dt = col_sb[:, 2:4]
        d_par = col_sb[:, 4:6]
        a_log = col_sb[:, 6:]
        a_neg = sb("a_neg", [P, HALVES, D_STATE])
        a_exp = sb("a_exp", [P, HALVES * D_STATE])
        w_in_sb = sb("w_in_sb", [P, 2 * D_INNER])
        tap_w = sb("tap_w", [P, D_CONV, D_INNER])
        w_x_sb = sb("w_x_sb", [P, HALVES, DT_RANK + 2 * D_STATE])
        w_dt_sb = sb("w_dt_sb", [DT_RANK, D_INNER])
        w_out_sb = sb("w_out_sb", [P, HALVES, D_MODEL])
        router_sb = sb("router_sb", [P, N_EXPERTS])
        bias_sb = sb("bias_sb", [P, N_EXPERTS])
        gate_sb = sb("gate_sb", [P, FFNS, D_FF])
        up_sb = sb("up_sb", [P, FFNS, D_FF])
        down_sb = sb("down_sb", [P, FFNS, 2, D_MODEL])
        ident = sb("ident", [P, P])
        rev = sb("rev", [P, N_EXPERTS])
        half_neg = sb("half_neg", [P, TILES])

        x = sb("x", [P, SEQS, TILES, D_MODEL])
        xn = sb("xn", [P, TILES, D_MODEL])
        xnt = sb("xnt", [P, PAD + TOKENS])
        xc = sb("xc", [P, 2, HALVES, TOKENS])
        gz = sb("gz", [P, 2, HALVES, TOKENS])
        dbl = sb("dbl", [DT_RANK + D_STATE, TOKENS])
        c_tok = sb("c_tok", [P, 2, TILES, D_STATE])
        sp_exp = sb("sp_exp", [P, HALVES, TOKENS])
        sp_relu = sb("sp_relu", [P, HALVES, TOKENS])
        dt = sb("dt", [P, HALVES, TOKENS])
        u = sb("u", [P, HALVES, TOKENS])
        b_all = sb("b_all", [P, D_STATE, TOKENS])
        conv_all = b_all[:, 0:2, :].rearrange("p a (b c) -> p (a b) c", c=D_INNER)
        da = sb("da", [P, DA_RING, HALVES, TOKENS])
        dbx = sb("dbx", [P, DA_RING, HALVES, TOKENS])
        h = sb("h", [P, 2, HALVES, TOKENS])
        acc = sb("acc", [P, 2, TILES, D_INNER])
        y = sb("y", [P, HALVES, TOKENS])
        x2 = sb("x2", [P, TILES, D_MODEL])
        x2t = sb("x2t", [P, 2, TOKENS])
        comb = sb("comb", [P, TILES, N_EXPERTS])
        comb_t = sb("comb_t", [N_EXPERTS, TOKENS])
        comb_all = sb("comb_all", [P, COMB_RING, TOKENS])
        xe = sb("xe", [P, 2, TOKENS])
        th = sb("th", [P, 2, TOKENS])
        up_cp = sb("up_cp", [P, 2, TOKENS])
        ga = sb("ga", [P, 2, TOKENS])
        hid = sb("hid", [P, 2, 2, TOKENS])
        out_sb = sb("out_sb", [P, TILES, D_MODEL])

        bn = {k: sb(f"bn_{k}", [P, TILES, 6]) for k in "abcf"}
        mv = {k: sb(f"mv_{k}", [P, TILES, 2]) for k in "abcf"}
        ve = {k: sb(f"ve_{k}", [P, TILES]) for k in "abcf"}
        rs = {k: sb(f"rs_{k}", [P, TILES]) for k in "abcf"}
        lg = sb("lg", [P, TILES, N_EXPERTS])
        ex = sb("ex", [P, TILES, N_EXPERTS])
        pr = sb("pr", [P, TILES, N_EXPERTS])
        eq = sb("eq", [P, TILES, N_EXPERTS])
        oh1 = sb("oh1", [P, TILES, N_EXPERTS])
        oh2 = sb("oh2", [P, TILES, N_EXPERTS])
        r_max = sb("r_max", [P, TILES])
        r_sum = sb("r_sum", [P, TILES])
        r_inv = sb("r_inv", [P, TILES])
        m1 = sb("m1", [P, TILES])
        m2 = sb("m2", [P, TILES])
        k1 = sb("k1", [P, TILES])
        k2 = sb("k2", [P, TILES])
        r_dif = sb("r_dif", [P, TILES])
        r_exp = sb("r_exp", [P, TILES])
        r_den = sb("r_den", [P, TILES])
        w1 = sb("w1", [P, TILES])
        w2 = sb("w2", [P, TILES])

        gate_ps = [bank("gate_ps0"), bank("gate_ps1")]
        up_ps = [bank("up_ps0"), bank("up_ps1")]
        down_ps = bank("down_ps")
        turn_ps = [bank("turn_ps0"), bank("turn_ps1")]
        misc_ps = bank("misc_ps")
        PRE_BANKS = {"xnt": misc_ps, "conv0": gate_ps[0], "conv1": up_ps[0], "gate0": gate_ps[1],
                     "gate1": up_ps[1], "dbl": turn_ps[0], "c": turn_ps[1], "dt0": down_ps, "dt1": misc_ps}

        def pre_bank(s, name):
            return PRE_BANKS[name] if s == 0 else misc_ps

        ld_x = [sem(f"ld_x{s}") for s in range(SEQS)]
        ld_cols = sem("ld_cols")
        ld_conv = sem("ld_conv")
        ld_w_in = sem("ld_w_in")
        ld_w_x = sem("ld_w_x")
        ld_w_dt = sem("ld_w_dt")
        ld_w_out = sem("ld_w_out")
        ld_router = sem("ld_router")
        ld_bias = sem("ld_bias")
        ld_gate = sem("ld_gate")
        ld_up = sem("ld_up")
        ld_down = sem("ld_down")
        b_stored = sem("b_stored")
        b_loaded = [sem(f"b_loaded{c}") for c in range(B_CHUNKS)]
        comb_stored = sem("comb_stored")
        comb_loaded = [sem(f"comb_loaded{c}") for c in range(2)]
        out_stored = sem("out_stored")

        ident_zero = sem("ident_zero")
        ident_ready = sem("ident_ready")
        consts_ready = sem("consts_ready")
        down_halved = sem("down_halved")
        ve_ready = sem("ve_ready")
        rs_ready = {k: sem(f"rs_ready_{k}") for k in "abcf"}
        u_ready = sem("u_ready")
        dbx_ready = sem("dbx_ready")
        y_ready = sem("y_ready")
        xe_ready = sem("xe_ready")
        hid_pool = sem("hid_pool")
        zeros_ready = sem("zeros_ready")
        taps_ready = sem("taps_ready")
        a_ready = sem("a_ready")
        dve_link = sem("dve_link")
        stats_ready = {k: sem(f"stats_ready_{k}") for k in "abcf"}
        xn_ready = sem("xn_ready")
        dt_ready = sem("dt_ready")
        scanned = sem("scanned")
        summed = sem("summed")
        y_added = sem("y_added")
        post_read = sem("post_read")
        x1_ready = sem("x1_ready")
        x2_ready = sem("x2_ready")
        lg_ready = sem("lg_ready")
        dif_ready = sem("dif_ready")
        comb_ready = sem("comb_ready")
        ga_ready = sem("ga_ready")
        hid_dve = sem("hid_dve")
        fin_read = sem("fin_read")
        out_ready = sem("out_ready")
        a_exp_ready = sem("a_exp_ready")
        xnt_ready = sem("xnt_ready")
        conv_ready = sem("conv_ready")
        gz_ready = sem("gz_ready")
        dbl_ready = sem("dbl_ready")
        c_ready = sem("c_ready")
        dt_read = sem("dt_read")
        sp_step = sem("sp_step")
        sp_ready = sem("sp_ready")
        da_ready = sem("da_ready")
        x2t_ready = sem("x2t_ready")
        ex_ready = sem("ex_ready")
        r_exp_ready = sem("r_exp_ready")
        comb_t_ready = sem("comb_t_ready")
        th_ready = sem("th_ready")
        up_ready = sem("up_ready")
        xn_turned = sem("xn_turned")
        conv_done = sem("conv_done")
        gate_done = sem("gate_done")
        dbl_done = sem("dbl_done")
        c_done = sem("c_done")
        dt_done = sem("dt_done")
        turned = sem("turned")
        acc_turned = sem("acc_turned")
        post_done = sem("post_done")
        x2_turned = sem("x2_turned")
        lg_done = sem("lg_done")
        comb_turned = sem("comb_turned")
        unit_done = sem("unit_done")
        down_done = sem("down_done")

        def pool_units(s, q):
            return s * sum(map(on_pool, range(UNITS))) + sum(map(on_pool, range(q)))

        def dve_units(s, q):
            return s * UNITS + q - pool_units(s, q)

        block = ctx.enter_context(nc.Block())

        @block.sync
        def _(sp):
            def store(s):
                sp.wait_ge(out_ready, s + 1)
                sp.dma_start(out[s], out_sb[:]).then_inc(out_stored, 16)

            sp.dma_start(x[:, 0], x_in[0]).then_inc(ld_x[0], 16)
            sp.dma_start(w_in_sb[:], w_in).then_inc(ld_w_in, 16)
            sp.dma_start(conv_all, conv_t.rearrange("(a k) c -> a k c", a=1)
                         .to_broadcast([P, D_CONV, D_INNER])).then_inc(ld_conv, 16)
            sp.dma_start(col_sb[:], cols).then_inc(ld_cols, 16)
            sp.dma_start(w_x_sb[:], w_x).then_inc(ld_w_x, 16)
            sp.dma_start(w_dt_sb[:], w_dt).then_inc(ld_w_dt, 16)
            for g in range(FIRST_SLOT, LAST_SLOT):
                if (s := pre_at(g, PRE_DBL)) is not None:
                    sp.wait_ge(dbl_ready, s + 1)
                    sp.dma_start(b_scratch[s], dbl[DT_RANK:, :]).then_inc(b_stored, 16)
                    sp.wait_ge(b_stored, 16 * (s + 1))
                    for c in range(B_CHUNKS):
                        n = B_CHUNK * c
                        if s == 0:
                            sp.wait_ge(taps_ready, D_CONV)
                        else:
                            sp.wait_ge(dbx_ready, D_STATE * (s - 1) + n + B_CHUNK)
                        sp.dma_start(b_all[:, n:n + B_CHUNK, :],
                                     b_scratch[s, n:n + B_CHUNK].rearrange("(a n) t -> a n t", a=1)
                                     .to_broadcast([P, B_CHUNK, TOKENS])).then_inc(b_loaded[c], 16)
                if g == PRE_DBL - D_STATE:
                    sp.dma_start(x[:, 1], x_in[1]).then_inc(ld_x[1], 16)
                    sp.dma_start(w_out_sb[:], w_out).then_inc(ld_w_out, 16)
                    sp.dma_start(router_sb[:], router_t).then_inc(ld_router, 16)
                    sp.dma_start(bias_sb[:], bias_r.rearrange("(a e) -> a e", a=1)
                                 .to_broadcast([P, N_EXPERTS])).then_inc(ld_bias, 16)
                    sp.dma_start(down_sb[:], down_t).then_inc(ld_down, 16)
                    sp.dma_start(gate_sb[:], gate_t).then_inc(ld_gate, 16)
                    sp.dma_start(up_sb[:], up_t).then_inc(ld_up, 16)
                    for i in range(2, SEQS):
                        sp.dma_start(x[:, i], x_in[i]).then_inc(ld_x[i], 16)
                if (s := post_at(g, ROUTE_C)) is not None:
                    sp.wait_ge(comb_t_ready, s + 1)
                    sp.dma_start(comb_scratch[s], comb_t[:]).then_inc(comb_stored, 16)
                    sp.wait_ge(comb_stored, 16 * (s + 1))
                    for c in range(N_EXPERTS // COMB_CHUNK):
                        e = COMB_CHUNK * c
                        if (used := N_EXPERTS * s + e + COMB_CHUNK - COMB_RING) > 0:
                            sp.wait_ge(xe_ready, used)
                        r = e % COMB_RING
                        sp.dma_start(comb_all[:, r:r + COMB_CHUNK, :],
                                     comb_scratch[s, e:e + COMB_CHUNK].rearrange("(a n) t -> a n t", a=1)
                                     .to_broadcast([P, COMB_CHUNK, TOKENS])).then_inc(comb_loaded[c % 2], 16)
                if (s := post_at(g, FIN_SLOT - D_STATE)) is not None and s >= 1:
                    store(s - 1)
            store(SEQS - 1)
            sp.wait_ge(out_stored, 16 * SEQS)

        @block.tensor
        def _(pe):
            def turn_states(m):
                pe.wait_ge(scanned, m + 1)
                for b in range(2):
                    if m >= 1:
                        pe.wait_ge(summed, TILES * (m - 1) + 2 * b + 2)
                    for t in range(2):
                        for c in range(HALVES):
                            tok = (2 * b + t) * P
                            last = nc.tensor.transpose(turn_ps[b][:, t * D_INNER + c * P:t * D_INNER + (c + 1) * P],
                                                       h[:, m % 2, c, tok:tok + P], ident[:])
                    last.then_inc(turned, 1)

            def gate_up(s, q):
                e, k = divmod(q, 2)
                v = UNITS * s + q
                if v == 0:
                    pe.wait_ge(ld_gate, 16)
                    pe.wait_ge(ld_up, 16)
                if q == 0:
                    pe.wait_ge(x2t_ready, s + 1)
                if e >= 1 and k == 0:
                    pe.wait_ge(xe_ready, N_EXPERTS * s + e)
                if v >= 2:
                    pe.wait_ge(ga_ready, v - 1)
                    s2, q2 = divmod(v - 2, UNITS)
                    if on_pool(q2):
                        pe.wait_ge(up_ready, pool_units(s2, q2) + 1)
                    else:
                        pe.wait_ge(hid_dve, dve_units(s2, q2) + 1)
                cols_k = slice(k * P, (k + 1) * P)
                nc.tensor.matmul(gate_ps[v % 2][:], gate_sb[:, e, cols_k], x2t[:, s % 2, :], start=True, stop=True)
                rhs = x2t[:, s % 2, :] if e == 0 else xe[:, e % 2, :]
                nc.tensor.matmul(up_ps[v % 2][:], up_sb[:, e, cols_k], rhs,
                                 start=True, stop=True).then_inc(unit_done, 1)

            def down(s, e):
                for k in range(2):
                    q = 2 * e + k
                    if on_pool(q):
                        pe.wait_ge(hid_pool, pool_units(s, q) + 1)
                    else:
                        pe.wait_ge(hid_dve, dve_units(s, q) + 1)
                if e == 0:
                    pe.wait_ge(down_halved, 1)
                    if s >= 1:
                        pe.wait_ge(fin_read, s)
                for t in range(TILES):
                    for k in range(2):
                        last = nc.tensor.matmul(down_ps[:, t * D_MODEL:(t + 1) * D_MODEL],
                                                hid[:, e % 2, k, t * P:(t + 1) * P], down_sb[:, e, k, :],
                                                start=(e == 0 and t == 0 and k == 0),
                                                stop=(e == FFNS - 1 and k == 1), skip_group_check=True)
                last.then_inc(down_done, 1)

            def turn_four(dst, src, width=P):
                for t in range(TILES):
                    last = nc.tensor.transpose(dst[0:width, t * P:(t + 1) * P], src[:, t, :], ident[:])
                return last

            for g in range(FIRST_SLOT, LAST_SLOT):
                if 1 <= g <= STEPS:
                    turn_states(g - 1)
                for s, q in units_at(g):
                    gate_up(s, q)
                    if q % 2 == 1 and q >= 3:
                        down(s, (q - 3) // 2)
                if (s := post_at(g, FIN_SLOT - D_STATE)) is not None and s >= 1:
                    down(s - 1, FFNS - 1)
                if g == STEPS + FIN_SLOT:
                    down(SEQS - 1, FFNS - 1)

                if (s := pre_at(g, PRE_NORM)) is not None:
                    pe.wait_ge(xn_ready, s + 1)
                    if s == 0:
                        pe.wait_ge(ident_ready, 1)
                    if s >= 2:
                        pe.wait_ge(comb_t_ready, s - 1)
                    elif s == 1:
                        pe.wait_ge(dt_read, 2)
                    turn_four(pre_bank(s, "xnt"), xn).then_inc(xn_turned, 1)
                if (s := pre_at(g, PRE_CONV)) is not None:
                    pe.wait_ge(xnt_ready, s + 1)
                    if s == 0:
                        pe.wait_ge(taps_ready, D_CONV)
                    for c in range(HALVES):
                        if s >= 1 and c == 1:
                            pe.wait_ge(conv_ready, HALVES * s + 1)
                        for k in range(D_CONV):
                            last = nc.tensor.matmul(pre_bank(s, f"conv{c}")[:], tap_w[:, k, c * P:(c + 1) * P],
                                                    xnt[:, k:k + TOKENS], start=(k == 0), stop=(k == D_CONV - 1))
                        last.then_inc(conv_done, 1)
                if (s := pre_at(g, PRE_GATE)) is not None:
                    for c in range(HALVES):
                        if s >= 1:
                            if c == 0:
                                pe.wait_ge(conv_ready, HALVES * (s + 1))
                            else:
                                pe.wait_ge(gz_ready, HALVES * s + 1)
                        nc.tensor.matmul(pre_bank(s, f"gate{c}")[:],
                                         w_in_sb[:, D_INNER + c * P:D_INNER + (c + 1) * P], xnt[:, PAD:],
                                         start=True, stop=True).then_inc(gate_done, 1)
                if (s := pre_at(g, PRE_DBL)) is not None:
                    pe.wait_ge(conv_ready, HALVES * (s + 1))
                    if s == 0:
                        pe.wait_ge(ld_w_x, 16)
                    else:
                        pe.wait_ge(gz_ready, HALVES * (s + 1))
                    rows = DT_RANK + D_STATE
                    for c in range(HALVES):
                        last = nc.tensor.matmul(pre_bank(s, "dbl")[0:rows, :], w_x_sb[:, c, 0:rows], xc[:, s % 2, c, :],
                                                start=(c == 0), stop=(c == HALVES - 1))
                    last.then_inc(dbl_done, 1)
                    if s >= 1:
                        pe.wait_ge(dbl_ready, s + 1)
                    for t in range(TILES):
                        for c in range(HALVES):
                            last = nc.tensor.matmul(pre_bank(s, "c")[:, t * D_STATE:(t + 1) * D_STATE],
                                                    xc[:, s % 2, c, t * P:(t + 1) * P], w_x_sb[:, c, rows:],
                                                    start=(c == 0), stop=(c == HALVES - 1))
                    last.then_inc(c_done, 1)
                if (s := pre_at(g, PRE_DT)) is not None:
                    pe.wait_ge(dbl_ready, s + 1)
                    if s == 0:
                        pe.wait_ge(ld_w_dt, 16)
                    else:
                        pe.wait_ge(c_ready, s + 1)
                    for c in range(HALVES):
                        if c == 1 and s >= 1:
                            pe.wait_ge(dt_read, 2 * s + 1)
                        nc.tensor.matmul(pre_bank(s, f"dt{c}")[:], w_dt_sb[:, c * P:(c + 1) * P],
                                         dbl[0:DT_RANK, :], start=True, stop=True).then_inc(dt_done, 1)

                if (s := post_at(g, POST_TURN)) is not None:
                    pe.wait_ge(summed, TILES * D_STATE * (s + 1))
                    pe.wait_ge(dt_read, 2 * min(s + 2, SEQS))
                    turn_four(misc_ps, acc[:, s % 2, :, 0:P]).then_inc(acc_turned, 1)
                if (s := post_at(g, POST_GATE)) is not None:
                    pe.wait_ge(y_added, HALVES * s + 1)
                    turn_four(misc_ps, acc[:, s % 2, :, P:]).then_inc(acc_turned, 1)
                    if s == 0:
                        pe.wait_ge(ld_w_out, 16)
                    pe.wait_ge(y_ready, HALVES * (s + 1))
                    for t in range(TILES):
                        for c in range(HALVES):
                            last = nc.tensor.matmul(misc_ps[:, t * D_MODEL:(t + 1) * D_MODEL],
                                                    y[:, c, t * P:(t + 1) * P], w_out_sb[:, c, :],
                                                    start=(c == 0), stop=(c == HALVES - 1))
                    last.then_inc(post_done, 1)
                if (s := post_at(g, POST_NORM)) is not None:
                    pe.wait_ge(post_read, s + 1)
                    pe.wait_ge(x2_ready, s + 1)
                    turn_four(misc_ps, x2).then_inc(x2_turned, 1)
                    pe.wait_ge(x2t_ready, s + 1)
                    if s == 0:
                        pe.wait_ge(ld_router, 16)
                    for t in range(TILES):
                        last = nc.tensor.matmul(misc_ps[:, t * N_EXPERTS:(t + 1) * N_EXPERTS],
                                                x2t[:, s % 2, t * P:(t + 1) * P], router_sb[:],
                                                start=True, stop=True)
                    last.then_inc(lg_done, 1)
                if (s := post_at(g, ROUTE_C)) is not None:
                    pe.wait_ge(comb_ready, s + 1)
                    turn_four(misc_ps, comb, N_EXPERTS).then_inc(comb_turned, 1)

        @block.scalar
        def _(act):
            def decay(m):
                s, n = divmod(m, D_STATE)
                if n == 0:
                    act.wait_ge(dt_ready, s + 1)
                if m == 0:
                    act.wait_ge(a_ready, 1)
                    act.wait_ge(zeros_ready, 2)
                if m >= DA_RING:
                    act.wait_ge(scanned, m - DA_RING + 1)
                for c in range(HALVES):
                    nc.scalar.activation(da[:, m % DA_RING, c, 1:], dt[:, c, 1:], ACT.Exp,
                                         scale=a_neg[:, c, n:n + 1]).then_inc(da_ready, 1)

            def gate_tanh(s, q):
                v = UNITS * s + q
                act.wait_ge(unit_done, v + 1)
                if v >= 2:
                    act.wait_ge(ga_ready, v - 1)
                nc.scalar.activation(th[:, v % 2, :], gate_ps[v % 2][:], ACT.Tanh, scale=0.5).then_inc(th_ready, 1)
                if on_pool(q):
                    i = pool_units(s, q)
                    if i >= 2:
                        act.wait_ge(hid_pool, i - 1)
                    nc.scalar.activation(up_cp[:, i % 2, :], up_ps[v % 2][:], ACT.Copy).then_inc(up_ready, 1)

            act.wait_ge(ld_cols, 16)
            nc.scalar.activation(a_exp[:], a_log, ACT.Exp).then_inc(a_exp_ready, 1)
            for g in range(FIRST_SLOT, LAST_SLOT):
                if 0 <= g + LEAD < STEPS:
                    decay(g + LEAD)
                for s, q in units_at(g):
                    gate_tanh(s, q)

                if (s := pre_at(g, PRE_NORM)) is not None:
                    act.wait_ge(xn_turned, s + 1)
                    if s == 0:
                        act.wait_ge(zeros_ready, 2)
                    else:
                        act.wait_ge(gate_done, HALVES * s)
                    nc.scalar.activation(xnt[:, PAD:], pre_bank(s, "xnt")[:], ACT.Copy).then_inc(xnt_ready, 1)
                if (s := pre_at(g, PRE_CONV)) is not None:
                    for c in range(HALVES):
                        act.wait_ge(conv_done, HALVES * s + c + 1)
                        if s >= 2:
                            act.wait_ge(y_added, HALVES * (s - 1))
                        nc.scalar.activation(xc[:, s % 2, c, :], pre_bank(s, f"conv{c}")[:], ACT.Silu,
                                             bias=conv_b[:, c:c + 1]).then_inc(conv_ready, 1)
                if (s := pre_at(g, PRE_GATE)) is not None:
                    for c in range(HALVES):
                        act.wait_ge(gate_done, HALVES * s + c + 1)
                        if s >= 2:
                            act.wait_ge(y_ready, HALVES * (s - 1))
                        nc.scalar.activation(gz[:, s % 2, c, :], pre_bank(s, f"gate{c}")[:],
                                             ACT.Silu).then_inc(gz_ready, 1)
                if (s := pre_at(g, PRE_DBL)) is not None:
                    act.wait_ge(dbl_done, s + 1)
                    if s >= 1:
                        act.wait_ge(b_stored, 16 * s)
                    nc.scalar.activation(dbl[:], pre_bank(s, "dbl")[0:DT_RANK + D_STATE, :],
                                         ACT.Copy).then_inc(dbl_ready, 1)
                    act.wait_ge(c_done, s + 1)
                    if s >= 2:
                        act.wait_ge(summed, TILES * D_STATE * (s - 1))
                    nc.scalar.activation(c_tok[:, s % 2], pre_bank(s, "c")[:, 0:TILES * D_STATE]
                                         .rearrange("p (t n) -> p t n", n=D_STATE), ACT.Copy).then_inc(c_ready, 1)
                if (s := pre_at(g, PRE_DT)) is not None:
                    if s >= 1:
                        act.wait_ge(dt_ready, s)
                    for c in range(HALVES):
                        act.wait_ge(dt_done, HALVES * s + c + 1)
                        nc.scalar.activation(sp_exp[:, c, :], pre_bank(s, f"dt{c}")[:], ACT.Abs,
                                             bias=b_dt[:, c:c + 1]).then_inc(sp_step, 1)
                        nc.scalar.activation(sp_relu[:, c, :], pre_bank(s, f"dt{c}")[:], ACT.Relu,
                                             bias=b_dt[:, c:c + 1]).then_inc(dt_read, 1)
                    act.wait_ge(sp_step, 3 * s + 2)
                    nc.scalar.activation(sp_exp[:], sp_exp[:], ACT.Exp, scale=-1.0).then_inc(sp_step, 1)
                    act.wait_ge(sp_step, 3 * s + 3)
                    nc.scalar.activation(sp_exp[:], sp_exp[:], ACT.Ln, bias=1.0).then_inc(sp_ready, 1)

                if (s := post_at(g, POST_NORM)) is not None:
                    act.wait_ge(x2_turned, s + 1)
                    if s >= 2:
                        act.wait_ge(unit_done, UNITS * (s - 1))
                    nc.scalar.activation(x2t[:, s % 2, :], misc_ps[:], ACT.Copy).then_inc(x2t_ready, 1)
                if (s := post_at(g, ROUTE_A)) is not None:
                    act.wait_ge(lg_ready, s + 1)
                    nc.scalar.activation(ex[:], lg[:], ACT.Exp).then_inc(ex_ready, 1)
                if (s := post_at(g, ROUTE_B)) is not None:
                    act.wait_ge(dif_ready, s + 1)
                    nc.scalar.activation(r_exp[:], r_dif[:], ACT.Exp).then_inc(r_exp_ready, 1)
                if (s := post_at(g, ROUTE_C)) is not None:
                    act.wait_ge(comb_turned, s + 1)
                    if s >= 1:
                        act.wait_ge(comb_stored, 16 * s)
                    nc.scalar.activation(comb_t[:], misc_ps[0:N_EXPERTS, :], ACT.Copy).then_inc(comb_t_ready, 1)

        @block.vector
        def _(dve):
            links = [0]

            def link(ins):
                links[0] += 1
                ins.then_inc(dve_link, 1)
                dve.wait_ge(dve_link, links[0])

            def stats(kind, tile):
                for t in range(TILES):
                    last = nc.vector.bn_stats(bn[kind][:, t, :], tile(t))
                link(last)
                for t in range(TILES):
                    last = nc.vector.bn_aggr(mv[kind][:, t, :], bn[kind][:, t, :])
                last.then_inc(stats_ready[kind], 1)

            def normalise(kind, s, dst, tile):
                dve.wait_ge(rs_ready[kind], s + 1)
                for t in range(TILES):
                    last = nc.vector.tensor_scalar(dst[:, t, :], tile(t), mv[kind][:, t, 0:1],
                                                   rs[kind][:, t:t + 1], ALU.subtract, ALU.mult)
                return last

            def scan(m):
                dve.wait_ge(da_ready, HALVES * (m + 1))
                dve.wait_ge(dbx_ready, m + 1)
                if m >= 2:
                    dve.wait_ge(turned, 2 * (m - 1))
                flat = lambda v: v.rearrange("p c t -> p (c t)")
                nc.vector.tensor_tensor_scan(flat(h[:, m % 2]), flat(da[:, m % DA_RING]), flat(dbx[:, m % DA_RING]),
                                             0.0, ALU.mult, ALU.add).then_inc(scanned, 1)

            def add_states(m):
                s, n = divmod(m, D_STATE)
                if n == 0:
                    dve.wait_ge(c_ready, s + 1)
                    if s >= 2:
                        dve.wait_ge(acc_turned, HALVES * (s - 1))
                for t in range(TILES):
                    if t % 2 == 0:
                        dve.wait_ge(turned, 2 * m + t // 2 + 1)
                    v = turn_ps[t // 2][:, (t % 2) * D_INNER:(t % 2 + 1) * D_INNER]
                    scalar = c_tok[:, s % 2, t, n:n + 1]
                    if n == 0:
                        last = nc.vector.tensor_scalar(acc[:, s % 2, t, :], v, scalar, None, ALU.mult)
                    else:
                        dve.wait_ge(summed, TILES * (m - 1) + t + 1)
                        last = nc.vector.scalar_tensor_tensor(out=acc[:, s % 2, t, :], in0=v, scalar=scalar,
                                                              in1=acc[:, s % 2, t, :], op0=ALU.mult, op1=ALU.add)
                    last.then_inc(summed, 1)

            def gate_mul(s, q):
                v = UNITS * s + q
                e, k = divmod(q, 2)
                dve.wait_ge(th_ready, v + 1)
                if v >= 2:
                    s2, q2 = divmod(v - 2, UNITS)
                    if on_pool(q2):
                        dve.wait_ge(hid_pool, pool_units(s2, q2) + 1)
                    else:
                        dve.wait_ge(hid_dve, dve_units(s2, q2) + 1)
                nc.vector.scalar_tensor_tensor(out=ga[:, v % 2, :], in0=th[:, v % 2, :], scalar=1.0,
                                               in1=gate_ps[v % 2][:], op0=ALU.add, op1=ALU.mult).then_inc(ga_ready, 1)
                if not on_pool(q):
                    dve.wait_ge(ga_ready, v + 1)
                    if FFNS * s + e >= 2:
                        dve.wait_ge(down_done, FFNS * s + e - 1)
                    nc.vector.tensor_tensor(hid[:, e % 2, k, :], ga[:, v % 2, :], up_ps[v % 2][:],
                                            ALU.mult).then_inc(hid_dve, 1)

            def finish_stats(s):
                dve.wait_ge(down_done, FFNS * (s + 1))
                stats("f", lambda t: down_ps[:, t * D_MODEL:(t + 1) * D_MODEL])

            def finish(s):
                if s >= 1:
                    dve.wait_ge(out_stored, 16 * s)
                normalise("f", s, out_sb,
                          lambda t: down_ps[:, t * D_MODEL:(t + 1) * D_MODEL]).then_inc(fin_read, 1)
                dve.wait_ge(fin_read, s + 1)
                nc.vector.tensor_tensor(out_sb[:], out_sb[:], x[:, s], ALU.add).then_inc(out_ready, 1)

            nc.vector.memset(da[:, :, :, 0:1], 0.0).then_inc(zeros_ready, 1)
            nc.vector.memset(xnt[:, 0:PAD], 0.0).then_inc(zeros_ready, 1)
            for g in range(FIRST_SLOT, LAST_SLOT):
                if 0 <= g < STEPS:
                    scan(g)
                if 1 <= g <= STEPS:
                    add_states(g - 1)
                for s, q in units_at(g):
                    gate_mul(s, q)

                if (s := pre_at(g, PRE_STATS)) is not None:
                    dve.wait_ge(ld_x[s], 16)
                    stats("a", lambda t: x[:, s, t, :])
                if (s := pre_at(g, PRE_NORM)) is not None:
                    if s >= 1:
                        dve.wait_ge(xn_turned, s)
                    normalise("a", s, xn, lambda t: x[:, s, t, :]).then_inc(xn_ready, 1)
                    if s == 0:
                        dve.wait_ge(ld_w_in, 16)
                        dve.wait_ge(ld_conv, 16)
                        for k in range(D_CONV):
                            nc.vector.tensor_tensor(tap_w[:, k, :], w_in_sb[:, 0:D_INNER], conv_all[:, k, :],
                                                    ALU.mult).then_inc(taps_ready, 1)
                        dve.wait_ge(a_exp_ready, 1)
                        nc.vector.tensor_scalar(a_neg[:].rearrange("p c n -> p (c n)"), a_exp[:], -1.0, None,
                                                ALU.mult).then_inc(a_ready, 1)
                if (s := pre_at(g, PRE_END)) is not None:
                    dve.wait_ge(sp_ready, s + 1)
                    dve.wait_ge(dt_read, HALVES * (s + 1))
                    if s >= 1:
                        dve.wait_ge(da_ready, HALVES * D_STATE * s)
                        dve.wait_ge(u_ready, s)
                    nc.vector.tensor_tensor(dt[:], sp_exp[:], sp_relu[:], ALU.add).then_inc(dt_ready, 1)

                if (s := post_at(g, POST_GATE)) is not None:
                    if s >= 1:
                        dve.wait_ge(post_done, s)
                    for c in range(HALVES):
                        dve.wait_ge(acc_turned, HALVES * s + c + 1)
                        nc.vector.scalar_tensor_tensor(out=y[:, c, :], in0=xc[:, s % 2, c, :], scalar=d_par[:, c:c + 1],
                                                       in1=misc_ps[:], op0=ALU.mult, op1=ALU.add).then_inc(y_added, 1)
                if (s := post_at(g, POST_STATS)) is not None:
                    dve.wait_ge(post_done, s + 1)
                    stats("b", lambda t: misc_ps[:, t * D_MODEL:(t + 1) * D_MODEL])
                if (s := post_at(g, POST_ADD)) is not None:
                    if s >= 1:
                        dve.wait_ge(x2_turned, s)
                    normalise("b", s, x2, lambda t: misc_ps[:, t * D_MODEL:(t + 1) * D_MODEL]).then_inc(post_read, 1)
                    dve.wait_ge(post_read, s + 1)
                    nc.vector.tensor_tensor(x[:, s], x[:, s], x2[:], ALU.add).then_inc(x1_ready, 1)
                    dve.wait_ge(x1_ready, s + 1)
                    stats("c", lambda t: x[:, s, t, :])
                if (s := post_at(g, POST_NORM)) is not None:
                    normalise("c", s, x2, lambda t: x[:, s, t, :]).then_inc(x2_ready, 1)
                if (s := post_at(g, ROUTE_A)) is not None:
                    dve.wait_ge(lg_done, s + 1)
                    if s == 0:
                        dve.wait_ge(ld_bias, 16)
                    wide = lambda v: v[:].rearrange("p (t a) -> p t a", a=1).to_broadcast([P, TILES, N_EXPERTS])
                    link(nc.vector.tensor_tensor(
                        lg[:], misc_ps[:, 0:TILES * N_EXPERTS].rearrange("p (t e) -> p t e", e=N_EXPERTS),
                        bias_sb[:].rearrange("p (a e) -> p a e", a=1).to_broadcast([P, TILES, N_EXPERTS]), ALU.add))
                    link(nc.vector.tensor_reduce(r_max[:], lg[:], AX_X, ALU.max))
                    nc.vector.tensor_tensor(lg[:], lg[:], wide(r_max), ALU.subtract).then_inc(lg_ready, 1)
                if (s := post_at(g, ROUTE_B)) is not None:
                    rev_wide = rev[:].rearrange("p (a e) -> p a e", a=1).to_broadcast([P, TILES, N_EXPERTS])

                    def first_of(best, key, onehot):
                        link(nc.vector.tensor_reduce(best[:], pr[:], AX_X, ALU.max))
                        link(nc.vector.tensor_tensor(eq[:], pr[:], wide(best), ALU.is_equal))
                        link(nc.vector.tensor_tensor(eq[:], eq[:], rev_wide, ALU.mult))
                        link(nc.vector.tensor_reduce(key[:], eq[:], AX_X, ALU.max))
                        link(nc.vector.tensor_tensor(onehot[:], rev_wide, wide(key), ALU.is_equal))

                    dve.wait_ge(ex_ready, s + 1)
                    dve.wait_ge(consts_ready, N_EXPERTS + 1)
                    link(nc.vector.tensor_reduce(r_sum[:], ex[:], AX_X, ALU.add))
                    link(nc.vector.reciprocal(r_inv[:], r_sum[:]))
                    link(nc.vector.tensor_tensor(pr[:], ex[:], wide(r_inv), ALU.mult))
                    first_of(m1, k1, oh1)
                    link(nc.vector.scalar_tensor_tensor(out=pr[:], in0=oh1[:], scalar=-4.0, in1=pr[:],
                                                        op0=ALU.mult, op1=ALU.add))
                    first_of(m2, k2, oh2)
                    nc.vector.tensor_tensor(r_dif[:], m2[:], m1[:], ALU.subtract).then_inc(dif_ready, 1)
                if (s := post_at(g, ROUTE_C)) is not None:
                    dve.wait_ge(r_exp_ready, s + 1)
                    link(nc.vector.tensor_scalar(r_den[:], r_exp[:], 1.0, None, ALU.add))
                    link(nc.vector.reciprocal(w1[:], r_den[:]))
                    link(nc.vector.tensor_tensor(w2[:], r_exp[:], w1[:], ALU.mult))
                    link(nc.vector.tensor_tensor(oh1[:], oh1[:], wide(w1), ALU.mult))
                    link(nc.vector.tensor_tensor(oh2[:], oh2[:], wide(w2), ALU.mult))
                    if s >= 1:
                        dve.wait_ge(comb_turned, s)
                    nc.vector.tensor_tensor(comb[:], oh1[:], oh2[:], ALU.add).then_inc(comb_ready, 1)
                if (s := post_at(g, FIN_SLOT - D_STATE)) is not None and s >= 1:
                    finish_stats(s - 1)
                if g == STEPS + FIN_SLOT:
                    finish_stats(SEQS - 1)
                if (s := post_at(g, FIN_SLOT + 1 - D_STATE)) is not None and s >= 1:
                    finish(s - 1)
                if g == STEPS + FIN_SLOT + 1:
                    finish(SEQS - 1)

        @block.gpsimd
        def _(pool):
            def rstd(kind, s):
                pool.wait_ge(stats_ready[kind], s + 1)
                rstds[0] += 1
                nc.gpsimd.tensor_scalar(ve[kind][:], mv[kind][:, :, 1], EPS, 1.0, ALU.add,
                                        ALU.mult).then_inc(ve_ready, 1)
                pool.wait_ge(ve_ready, rstds[0])
                nc.gpsimd.tensor_tensor(rs[kind][:], ve[kind][:], half_neg[:], ALU.pow).then_inc(rs_ready[kind], 1)

            def inject(m):
                s, n = divmod(m, D_STATE)
                if n == 0:
                    pool.wait_ge(u_ready, s + 1)
                if n % B_CHUNK == 0:
                    pool.wait_ge(b_loaded[n // B_CHUNK], 16 * (s + 1))
                if m >= DA_RING:
                    pool.wait_ge(scanned, m - DA_RING + 1)
                nc.gpsimd.tensor_tensor(dbx[:, m % DA_RING], u[:],
                                        b_all[:, n:n + 1, :].to_broadcast([P, HALVES, TOKENS]),
                                        ALU.mult).then_inc(dbx_ready, 1)

            def scale_up(s, e):
                if e == 0:
                    pool.wait_ge(x2t_ready, s + 1)
                if e % COMB_CHUNK == 0:
                    c = e // COMB_CHUNK
                    pool.wait_ge(comb_loaded[c % 2], 16 * (2 * s + c // 2 + 1))
                if (v := UNITS * s + 2 * (e + 1)) - UNITS * s > 4:
                    pool.wait_ge(unit_done, v - 2)
                elif s >= 1:
                    pool.wait_ge(unit_done, UNITS * s)
                nc.gpsimd.tensor_tensor(xe[:, (e + 1) % 2, :], x2t[:, s % 2, :], comb_all[:, e % COMB_RING, :],
                                        ALU.mult).then_inc(xe_ready, 1)

            def mul_up(s, q):
                v = UNITS * s + q
                e, k = divmod(q, 2)
                pool.wait_ge(ga_ready, v + 1)
                i = pool_units(s, q)
                pool.wait_ge(up_ready, i + 1)
                if FFNS * s + e >= 2:
                    pool.wait_ge(down_done, FFNS * s + e - 1)
                nc.gpsimd.tensor_tensor(hid[:, e % 2, k, :], ga[:, v % 2, :], up_cp[:, i % 2, :],
                                        ALU.mult).then_inc(hid_pool, 1)

            rstds = [0]
            nc.gpsimd.memset(ident[:], 0.0).then_inc(ident_zero, 1)
            nc.gpsimd.memset(half_neg[:], -0.5).then_inc(consts_ready, 1)
            for e in range(N_EXPERTS):
                nc.gpsimd.memset(rev[:, e:e + 1], float(N_EXPERTS - e)).then_inc(consts_ready, 1)
            pool.wait_ge(ident_zero, 1)
            nc.gpsimd.affine_select(out=ident[:], in_=ident[:], compare_op=ALU.not_equal, fill=1.0, base=0,
                                    pattern=[[-1, P]], channel_multiplier=1).then_inc(ident_ready, 1)
            pool.wait_ge(consts_ready, N_EXPERTS + 1)
            for g in range(FIRST_SLOT, LAST_SLOT):
                if 0 <= g + LEAD < STEPS:
                    inject(g + LEAD)
                for s, q in units_at(g):
                    if on_pool(q):
                        mul_up(s, q)
                    if q % 2 == 0 and q // 2 < N_EXPERTS:
                        scale_up(s, q // 2)

                if g == D_STATE // 2:
                    pool.wait_ge(ld_down, 16)
                    flat = down_sb[:].rearrange("p e k d -> p (e k d)")
                    nc.gpsimd.tensor_scalar(flat, flat, 0.5, 1.0, ALU.mult, ALU.mult).then_inc(down_halved, 1)
                if (s := pre_at(g, PRE_STATS)) is not None:
                    rstd("a", s)
                if (s := pre_at(g, PRE_END)) is not None:
                    pool.wait_ge(dt_ready, s + 1)
                    pool.wait_ge(conv_ready, HALVES * (s + 1))
                    if s >= 1:
                        pool.wait_ge(dbx_ready, D_STATE * s)
                    nc.gpsimd.tensor_tensor(u[:], dt[:], xc[:, s % 2], ALU.mult).then_inc(u_ready, 1)
                if (s := post_at(g, POST_GATE)) is not None:
                    for c in range(HALVES):
                        pool.wait_ge(y_added, HALVES * s + c + 1)
                        pool.wait_ge(gz_ready, HALVES * s + c + 1)
                        nc.gpsimd.tensor_tensor(y[:, c, :], y[:, c, :], gz[:, s % 2, c, :],
                                                ALU.mult).then_inc(y_ready, 1)
                if (s := post_at(g, POST_STATS)) is not None:
                    rstd("b", s)
                if (s := post_at(g, POST_ADD)) is not None:
                    rstd("c", s)
                if (s := post_at(g, FIN_SLOT - D_STATE)) is not None and s >= 1:
                    rstd("f", s - 1)
                if g == STEPS + FIN_SLOT:
                    rstd("f", SEQS - 1)


def kernel(**inputs):
    import numpy as np
    import concourse.bacc as bacc
    from concourse.bass_utils import run_bass_kernel_spmd

    a = {k.removeprefix("L0_"): np.asarray(v) for k, v in inputs.items()}

    def channels(v):
        return np.moveaxis(v.reshape(HALVES, P, *v.shape[1:]), 0, 1)

    def with_shared(shared, experts, axes):
        return np.ascontiguousarray(np.concatenate([shared[None], experts]).transpose(axes))

    arrays = {
        "x_in": np.ascontiguousarray(a["attn_x"].reshape(SEQS, TILES, P, D_MODEL).transpose(0, 2, 1, 3)),
        "cols": np.ascontiguousarray(np.concatenate(
            [channels(a["attn_conv_b"]), channels(a["attn_b_dt"]), channels(a["attn_D_param"]),
             channels(a["attn_A_log"]).reshape(P, HALVES * D_STATE)], axis=1)),
        "w_in": np.ascontiguousarray(a["attn_W_in"]),
        "conv_t": np.ascontiguousarray(a["attn_conv_w"].T),
        "w_x": np.ascontiguousarray(channels(a["attn_W_x"])),
        "w_dt": np.ascontiguousarray(a["attn_W_dt"]),
        "w_out": np.ascontiguousarray(channels(a["attn_W_out"])),
        "router_t": np.ascontiguousarray(a["ffn_router_w"].T),
        "bias_r": np.ascontiguousarray(a["ffn_expert_bias"]),
        "gate_t": with_shared(a["ffn_sw_gate"], a["ffn_ew_gate"], (2, 0, 1)),
        "up_t": with_shared(a["ffn_sw_up"], a["ffn_ew_up"], (2, 0, 1)),
        "down_t": np.ascontiguousarray(np.concatenate([a["ffn_sw_down"][None], a["ffn_ew_down"]])
                                       .reshape(FFNS, D_MODEL, 2, P).transpose(3, 0, 2, 1)),
    }
    nc = bacc.Bacc("TRN2", target_bir_lowering=False, num_devices=1)
    args = [nc.dram_tensor(k, v.shape, F32, kind="ExternalInput").ap() for k, v in arrays.items()]
    b_scratch = nc.dram_tensor("b_scratch", (SEQS, D_STATE, TOKENS), F32, kind="Internal").ap()
    comb_scratch = nc.dram_tensor("comb_scratch", (SEQS, N_EXPERTS, TOKENS), F32, kind="Internal").ap()
    out = nc.dram_tensor("out", (SEQS, P, TILES, D_MODEL), F32, kind="ExternalOutput").ap()
    build(nc, *args, b_scratch, comb_scratch, out)
    r = run_bass_kernel_spmd(nc, [arrays], core_ids=[0])
    got = np.asarray(r.results[0]["out"])
    return np.ascontiguousarray(got.transpose(0, 2, 1, 3)).reshape(SEQS, TOKENS, D_MODEL)
```

```python
from contextlib import ExitStack

import concourse.bass as bass
from concourse import mybir

F32 = mybir.dt.float32
F32R = mybir.dt.float32r
ALU = mybir.AluOpType
ACT = mybir.ActivationFunctionType
AX_X = mybir.AxisListType.X

P = 128
SEQS, TOKENS, D_MODEL = 4, 512, 128
D_INNER, D_STATE, D_CONV, DT_RANK = 256, 16, 4, 64
DBL_ROWS = DT_RANK + 2 * D_STATE
HALVES = D_INNER // P
TILES = TOKENS // P
N_EXPERTS, D_FF = 8, 256
FFNS = N_EXPERTS + 1
PAD = D_CONV - 1
EPS = 1e-5

STEPS = SEQS * D_STATE
LEAD = 2
DA_RING = LEAD + 1
B_CHUNK = 4
B_CHUNKS = D_STATE // B_CHUNK
UNITS = FFNS * 2
B_RING = 8
SPLIT_PIECES = 4
FFN_COLS = FFNS * D_FF

(PRE_STATS, PRE_NORM, PRE_TURN, PRE_CONV0, PRE_CONV1, PRE_CONV2, PRE_CONV3, PRE_DBL, PRE_DT, PRE_END, PRE_GATE) = (4, 5, 6, 7, 7, 8, 8, 9, 10, 13, 13)
(POST_TURN, POST_GATE, POST_STATS, POST_ADD, POST_NORM, POST_LOGITS, ROUTE_A, ROUTE_B, ROUTE_C) = (0, 1, 2, 3, 4, 5, 5, 8, 10)
UNITS_A = (1, 1, 2, 0, 2, 0, 2, 1, 1, 2, 2, 0, 2, 0, 0, 2)
UNITS_B = (1, 1, 2, 1, 1, 0, 1, 2, 1, 2, 1, 0, 2, 2, 0, 1, 0)
UNITS_C = (1, 1, 2, 2, 2, 2, 1, 2, 2, 3)
DOWNS_A = (0, 0, 0, 0, 0, 1, 1, 1, 0, 1, 1, 1, 0, 1, 0, 1, 0, 0, 1)
DOWNS_B = (0, 0, 0, 0, 1, 1, 0, 1, 0, 1, 1, 0, 1, 1, 1, 0, 0, 1, 0)
DOWNS_C = (0, 0, 1, 0, 1, 1, 1, 1, 1, 0, 2, 0, 1)


def spread(counts):
    return [POST_LOGITS + i for i, c in enumerate(counts) for _ in range(c)]


UNIT_SLOTS = [spread(UNITS_A)] * (SEQS - 2) + [spread(UNITS_B), spread(UNITS_C)]
DOWN_SLOTS = [spread(DOWNS_A)] * (SEQS - 2) + [spread(DOWNS_B), spread(DOWNS_C)]
FIN_STATS, FIN_OUT = (3, 6)
POOL_UNITS = (1, 1, 0, 1, 1, 0, 1, 0, 1, 0, 0, 0, 1, 0, 1, 1, 1, 0)
FIRST_SLOT = PRE_STATS - D_STATE
LAST_SLOT = STEPS + DOWN_SLOTS[-1][-1] + FIN_OUT + 1


def pre_at(g, stage):
    s, r = divmod(g - stage + D_STATE, D_STATE)
    return s if r == 0 and 0 <= s < SEQS else None


def post_at(g, stage):
    s, r = divmod(g - stage, D_STATE)
    return s - 1 if r == 0 and 1 <= s <= SEQS else None


def fin_at(g, stage):
    return next((s for s in range(SEQS) if D_STATE * (s + 1) + DOWN_SLOTS[s][-1] + stage == g), None)


def units_at(g):
    return [(s, q) for s in range(SEQS) for q in range(UNITS) if D_STATE * (s + 1) + UNIT_SLOTS[s][q] == g]


def downs_at(g):
    return [(s, e) for s in range(SEQS) for e in range(FFNS) if D_STATE * (s + 1) + DOWN_SLOTS[s][e] == g]


def on_pool(q):
    return POOL_UNITS[q] == 1


def build(nc, x_in, cols, w_in, conv_t, w_x, w_dt, w_out, router_t, bias_r, gate_t, up_t, down_t,
          b_scratch, out):
    with ExitStack() as ctx:
        def sb(name, shape, dt=F32):
            return ctx.enter_context(nc.sbuf_tensor(name, shape, dt))

        def bank(name):
            return ctx.enter_context(nc.psum_tensor(name, [P, TOKENS], F32))

        def sem(name):
            return ctx.enter_context(nc.semaphore(name))

        col_sb = sb("col_sb", [P, 3 * HALVES + HALVES * D_STATE])
        conv_b = col_sb[:, 0:2]
        b_dt = col_sb[:, 2:4]
        d_par = col_sb[:, 4:6]
        a_log = col_sb[:, 6:]
        a_neg = sb("a_neg", [P, HALVES, D_STATE])
        a_exp = sb("a_exp", [P, HALVES * D_STATE])
        tap_hi = sb("tap_hi", [P, D_CONV, D_INNER], F32R)
        tap_lo = sb("tap_lo", [P, D_CONV, D_INNER], F32R)
        gate_w_hi = sb("gate_w_hi", [P, D_INNER], F32R)
        gate_w_lo = sb("gate_w_lo", [P, D_INNER], F32R)
        w_x_sb = sb("w_x_sb", [P, HALVES, DT_RANK + 2 * D_STATE])
        w_dt_sb = sb("w_dt_sb", [DT_RANK, D_INNER])
        w_out_sb = sb("w_out_sb", [P, HALVES, D_MODEL])
        router_sb = sb("router_sb", [P, N_EXPERTS])
        router_hi = sb("router_hi", [P, N_EXPERTS], F32R)
        router_lo = sb("router_lo", [P, N_EXPERTS], F32R)
        bias_sb = sb("bias_sb", [P, N_EXPERTS])
        ffn_hi = sb("ffn_hi", [P, 2, FFN_COLS], F32R)
        ffn_lo = sb("ffn_lo", [P, 2, FFN_COLS], F32R)
        down_sb = sb("down_sb", [P, FFNS, 2, D_MODEL])
        ident = sb("ident", [P, P])
        rev = sb("rev", [P, N_EXPERTS])
        half_neg = sb("half_neg", [P, TILES])

        x = sb("x", [P, SEQS, TILES, D_MODEL])
        xn = sb("xn", [P, TILES, D_MODEL])
        xnt_hi = sb("xnt_hi", [P, PAD + TOKENS], F32R)
        xnt_lo = sb("xnt_lo", [P, PAD + TOKENS], F32R)
        xc = sb("xc", [P, 2, HALVES, TOKENS])
        gz = sb("gz", [P, 2, HALVES, TOKENS])
        dbl = sb("dbl", [DBL_ROWS, TOKENS])
        c_tok = sb("c_tok", [P, 2, TILES, D_STATE])
        sp_exp = sb("sp_exp", [P, HALVES, TOKENS])
        sp_relu = sb("sp_relu", [P, HALVES, TOKENS])
        dt = sb("dt", [P, HALVES, TOKENS])
        u = sb("u", [P, HALVES, TOKENS])
        b_all = sb("b_all", [P, B_RING, TOKENS])
        da = sb("da", [P, DA_RING, HALVES, TOKENS])
        dbx = sb("dbx", [P, DA_RING, HALVES, TOKENS])
        h = sb("h", [P, 2, HALVES, TOKENS])
        acc = sb("acc", [P, 2, TILES, D_INNER])
        y = sb("y", [P, HALVES, TOKENS])
        x2 = sb("x2", [P, TILES, D_MODEL])
        x2t_hi = sb("x2t_hi", [P, 2, TOKENS], F32R)
        x2t_lo = sb("x2t_lo", [P, 2, TOKENS], F32R)
        comb = sb("comb", [P, 2, TILES, N_EXPERTS])
        ffn_sum = sb("ffn_sum", [P, 2, TILES, D_MODEL])
        ffn_one = sb("ffn_one", [P, 2, TILES, D_MODEL])
        work = sb("work", [P, 10, TOKENS])
        th, up_cp, ga = (work[:, 2 * i:2 * i + 2, :] for i in range(3))
        hid = work[:, 6:10, :].rearrange("p (e k) t -> p e k t", k=2)
        flat_work = work[:].rearrange("p a t -> p (a t)")
        w_in_raw = flat_work[:, 0:2 * D_INNER]
        conv_raw = flat_work[:, 2 * D_INNER:(2 + D_CONV) * D_INNER].rearrange("p (k c) -> p k c", k=D_CONV)
        tap_raw = flat_work[:, (2 + D_CONV) * D_INNER:(2 + 2 * D_CONV) * D_INNER].rearrange("p (k c) -> p k c", k=D_CONV)
        ffn_raw = flat_work[:, 0:2 * FFN_COLS]

        bn = {k: sb(f"bn_{k}", [P, TILES, 6]) for k in "abcf"}
        mv = {k: sb(f"mv_{k}", [P, TILES, 2]) for k in "abcf"}
        ve = {k: sb(f"ve_{k}", [P, TILES]) for k in "abcf"}
        rs = {k: sb(f"rs_{k}", [P, TILES]) for k in "abcf"}
        lg = sb("lg", [P, TILES, N_EXPERTS])
        ex = sb("ex", [P, TILES, N_EXPERTS])
        pr = sb("pr", [P, TILES, N_EXPERTS])
        eq = sb("eq", [P, TILES, N_EXPERTS])
        oh1 = sb("oh1", [P, TILES, N_EXPERTS])
        oh2 = sb("oh2", [P, TILES, N_EXPERTS])
        r_max = sb("r_max", [P, TILES])
        r_sum = sb("r_sum", [P, TILES])
        r_inv = sb("r_inv", [P, TILES])
        m1 = sb("m1", [P, TILES])
        m2 = sb("m2", [P, TILES])
        k1 = sb("k1", [P, TILES])
        k2 = sb("k2", [P, TILES])
        r_dif = sb("r_dif", [P, TILES])
        r_exp = sb("r_exp", [P, TILES])
        r_den = sb("r_den", [P, TILES])
        w1 = sb("w1", [P, TILES])
        w2 = sb("w2", [P, TILES])

        gate_ps = [bank("gate_ps0"), bank("gate_ps1")]
        up_ps = [bank("up_ps0"), bank("up_ps1")]
        down_ps = bank("down_ps")
        turn_ps = [bank("turn_ps0"), bank("turn_ps1")]
        misc_ps = bank("misc_ps")
        PRE_BANKS = {"xnt": misc_ps, "conv0": gate_ps[0], "conv1": up_ps[0], "gate0": gate_ps[1],
                     "gate1": up_ps[1], "dbl": turn_ps[0], "c": turn_ps[1], "dt0": down_ps, "dt1": misc_ps}

        def pre_bank(s, name):
            return PRE_BANKS[name] if s == 0 else misc_ps

        ld_x = [sem(f"ld_x{s}") for s in range(SEQS)]
        ld_cols = sem("ld_cols")
        ld_conv = sem("ld_conv")
        ld_w_in = sem("ld_w_in")
        ld_w_x = sem("ld_w_x")
        ld_w_dt = sem("ld_w_dt")
        ld_w_out = sem("ld_w_out")
        ld_router = sem("ld_router")
        ld_bias = sem("ld_bias")
        ld_ffn = [sem("ld_gate_w"), sem("ld_up_w")]
        ld_down = sem("ld_down")
        b_stored = sem("b_stored")
        b_loaded = [sem(f"b_loaded{c}") for c in range(2)]
        out_stored = [sem(f"out_stored{i}") for i in range(2)]

        ident_zero = sem("ident_zero")
        ident_ready = sem("ident_ready")
        consts_ready = sem("consts_ready")
        rs_ready = {k: sem(f"rs_ready_{k}") for k in "abcf"}
        u_ready = sem("u_ready")
        dbx_ready = sem("dbx_ready")
        y_ready = sem("y_ready")
        ffn_added = sem("ffn_added")
        hid_pool = sem("hid_pool")
        zeros_ready = sem("zeros_ready")
        w_in_hi = sem("w_in_hi")
        taps_raw = sem("taps_raw")
        taps_hi = sem("taps_hi")
        w_in_ready = sem("w_in_ready")
        router_split = sem("router_split")
        ffn_w_ready = sem("ffn_w_ready")
        xnt_lo_ready = sem("xnt_lo_ready")
        x2t_lo_ready = sem("x2t_lo_ready")
        a_ready = sem("a_ready")
        dve_link = sem("dve_link")
        stats_ready = {k: sem(f"stats_ready_{k}") for k in "abcf"}
        xn_ready = sem("xn_ready")
        dt_ready = sem("dt_ready")
        first_dbx = sem("first_dbx")
        scanned = sem("scanned")
        summed = sem("summed")
        y_added = sem("y_added")
        post_read = sem("post_read")
        x1_ready = sem("x1_ready")
        x2_ready = sem("x2_ready")
        lg_ready = sem("lg_ready")
        dif_ready = sem("dif_ready")
        comb_ready = sem("comb_ready")
        ga_ready = sem("ga_ready")
        hid_dve = sem("hid_dve")
        fin_scaled = sem("fin_scaled")
        out_ready = sem("out_ready")
        a_exp_ready = sem("a_exp_ready")
        xnt_hi_ready = sem("xnt_hi_ready")
        ffn_w_hi = sem("ffn_w_hi")
        conv_ready = sem("conv_ready")
        gz_ready = sem("gz_ready")
        dbl_ready = sem("dbl_ready")
        c_ready = sem("c_ready")
        dt_read = sem("dt_read")
        sp_step = sem("sp_step")
        sp_ready = sem("sp_ready")
        da_ready = sem("da_ready")
        x2t_hi_ready = sem("x2t_hi_ready")
        ex_ready = sem("ex_ready")
        r_exp_ready = sem("r_exp_ready")
        ffn_moved = sem("ffn_moved")
        th_ready = sem("th_ready")
        up_ready = sem("up_ready")
        xn_turned = sem("xn_turned")
        conv_done = sem("conv_done")
        gate_done = sem("gate_done")
        dbl_done = sem("dbl_done")
        c_turned = sem("c_turned")
        dt_done = sem("dt_done")
        turned = sem("turned")
        acc_turned = sem("acc_turned")
        post_done = sem("post_done")
        x2_turned = sem("x2_turned")
        lg_done = sem("lg_done")
        unit_done = sem("unit_done")
        down_done = sem("down_done")

        def pool_units(s, q):
            return s * sum(map(on_pool, range(UNITS))) + sum(map(on_pool, range(q)))

        def dve_units(s, q):
            return s * UNITS + q - pool_units(s, q)

        def split_piece(g):
            c, r = divmod(g - 3, 2)
            return c if r == 0 and 0 <= c < SPLIT_PIECES else None

        def pieces(tile, c):
            size = 2 * FFN_COLS // SPLIT_PIECES
            flat = tile if tile is ffn_raw else tile[:].rearrange("p a c -> p (a c)")
            return flat[:, c * size:(c + 1) * size]

        block = ctx.enter_context(nc.Block())

        @block.sync
        def _(sp):
            def load_b(s, c):
                i = B_CHUNKS * s + c
                if i >= 2:
                    sp.wait_ge(dbx_ready, B_CHUNK * (i - 1) - 1)
                r = B_CHUNK * (i % 2)
                sp.dma_start(b_all[:, r:r + B_CHUNK, :],
                             b_scratch[s, B_CHUNK * c:B_CHUNK * (c + 1)].rearrange("(a n) t -> a n t", a=1)
                             .to_broadcast([P, B_CHUNK, TOKENS])).then_inc(b_loaded[i % 2], 16)

            def store(s):
                sp.wait_ge(out_ready, s + 1)
                sp.dma_start(out[s], ffn_sum[:, s % 2]).then_inc(out_stored[s % 2], 16)

            sp.dma_start(x[:, 0], x_in[0]).then_inc(ld_x[0], 16)
            sp.dma_start(w_in_raw, w_in).then_inc(ld_w_in, 16)
            sp.dma_start(conv_raw, conv_t.rearrange("(a k) c -> a k c", a=1)
                         .to_broadcast([P, D_CONV, D_INNER])).then_inc(ld_conv, 16)
            sp.dma_start(col_sb[:], cols).then_inc(ld_cols, 16)
            sp.dma_start(w_x_sb[:], w_x).then_inc(ld_w_x, 16)
            sp.dma_start(w_dt_sb[:], w_dt).then_inc(ld_w_dt, 16)
            for g in range(FIRST_SLOT, LAST_SLOT):
                if (s := pre_at(g, PRE_DBL)) is not None:
                    sp.wait_ge(dbl_ready, s + 1)
                    sp.dma_start(b_scratch[s], dbl[DT_RANK + D_STATE:, :]).then_inc(b_stored, 16)
                    sp.wait_ge(b_stored, 16 * (s + 1))
                    load_b(s, 0)
                if (s := pre_at(g, PRE_END)) is not None:
                    load_b(s, 1)
                if g == PRE_DBL - D_STATE:
                    sp.dma_start(x[:, 1], x_in[1]).then_inc(ld_x[1], 16)
                    sp.dma_start(w_out_sb[:], w_out).then_inc(ld_w_out, 16)
                    sp.dma_start(router_sb[:], router_t).then_inc(ld_router, 16)
                    sp.dma_start(bias_sb[:], bias_r.rearrange("(a e) -> a e", a=1)
                                 .to_broadcast([P, N_EXPERTS])).then_inc(ld_bias, 16)
                    sp.wait_ge(w_in_ready, 2)
                    for i in range(2):
                        sp.dma_start(ffn_raw[:, i * FFN_COLS:(i + 1) * FFN_COLS],
                                     (gate_t, up_t)[i].rearrange("d e f -> d (e f)")).then_inc(ld_ffn[i], 16)
                    sp.dma_start(down_sb[:], down_t).then_inc(ld_down, 16)
                    for i in range(2, SEQS):
                        sp.dma_start(x[:, i], x_in[i]).then_inc(ld_x[i], 16)
                for c in (2, 3):
                    if 0 <= g < STEPS and g % D_STATE == B_CHUNK * (c - 1) - LEAD:
                        load_b(g // D_STATE, c)
                if (s := fin_at(g, FIN_OUT)) is not None:
                    store(s)
            for stored in out_stored:
                sp.wait_ge(stored, 16 * (SEQS // 2))

        @block.tensor
        def _(pe):
            def turn_states(m):
                pe.wait_ge(scanned, m + 1)
                for b in range(2):
                    if m >= 1:
                        pe.wait_ge(summed, TILES * (m - 1) + 2 * b + 2)
                    for t in range(2):
                        for c in range(HALVES):
                            tok = (2 * b + t) * P
                            last = nc.tensor.transpose(turn_ps[b][:, t * D_INNER + c * P:t * D_INNER + (c + 1) * P],
                                                       h[:, m % 2, c, tok:tok + P], ident[:])
                    last.then_inc(turned, 1)

            def three(dst, pairs, start=True, stop=True):
                for i, ((w_hi, w_lo), (v_hi, v_lo)) in enumerate(pairs):
                    for j, (w, v) in enumerate(((w_hi, v_hi), (w_hi, v_lo), (w_lo, v_hi))):
                        last = nc.tensor.matmul(dst, w, v, start=(start and i == 0 and j == 0),
                                                stop=(stop and i == len(pairs) - 1 and j == 2))
                return last

            def gate_up(s, q):
                e, k = divmod(q, 2)
                v = UNITS * s + q
                if v == 0:
                    pe.wait_ge(ffn_w_ready, SPLIT_PIECES)
                if q == 0:
                    pe.wait_ge(x2t_lo_ready, s + 1)
                if v >= 2:
                    pe.wait_ge(ga_ready, v - 1)
                    s2, q2 = divmod(v - 2, UNITS)
                    if on_pool(q2):
                        pe.wait_ge(up_ready, pool_units(s2, q2) + 1)
                    else:
                        pe.wait_ge(hid_dve, dve_units(s2, q2) + 1)
                x2t_both = (x2t_hi[:, s % 2, :], x2t_lo[:, s % 2, :])
                col = e * D_FF + k * P
                for i, ps in enumerate((gate_ps, up_ps)):
                    last = three(ps[v % 2][:], [((ffn_hi[:, i, col:col + P], ffn_lo[:, i, col:col + P]), x2t_both)])
                last.then_inc(unit_done, 1)

            def down(s, e):
                for k in range(2):
                    q = 2 * e + k
                    if on_pool(q):
                        pe.wait_ge(hid_pool, pool_units(s, q) + 1)
                    else:
                        pe.wait_ge(hid_dve, dve_units(s, q) + 1)
                i = FFNS * s + e
                if i == 0:
                    pe.wait_ge(ld_down, 16)
                else:
                    pe.wait_ge(ffn_moved, i)
                for t in range(TILES):
                    for k in range(2):
                        last = nc.tensor.matmul(down_ps[:, t * D_MODEL:(t + 1) * D_MODEL],
                                                hid[:, (FFNS * s + e) % 2, k, t * P:(t + 1) * P], down_sb[:, e, k, :],
                                                start=(k == 0), stop=(k == 1))
                last.then_inc(down_done, 1)

            def turn_four(dst, src, width=P):
                for t in range(TILES):
                    last = nc.tensor.transpose(dst[0:width, t * P:(t + 1) * P], src[:, t, :], ident[:])
                return last

            def gate_z(s):
                for c in range(HALVES):
                    if s >= 1:
                        if c == 0:
                            pe.wait_ge(dt_read, HALVES * (s + 1))
                        else:
                            pe.wait_ge(gz_ready, HALVES * s + 1)
                    ch = slice(c * P, (c + 1) * P)
                    three(pre_bank(s, f"gate{c}")[:],
                          [((gate_w_hi[:, ch], gate_w_lo[:, ch]), (xnt_hi[:, PAD:], xnt_lo[:, PAD:]))]
                          ).then_inc(gate_done, 1)

            for g in range(FIRST_SLOT, LAST_SLOT):
                if 1 <= g <= STEPS:
                    turn_states(g - 1)
                if (s := pre_at(g, PRE_TURN)) is not None:
                    pe.wait_ge(xn_ready, s + 1)
                    if s == 0:
                        pe.wait_ge(ident_ready, 1)
                    elif s == 1:
                        pe.wait_ge(dt_read, HALVES)
                    else:
                        pe.wait_ge(lg_ready, s - 1)
                    turn_four(pre_bank(s, "xnt"), xn).then_inc(xn_turned, 1)
                for s, q in units_at(g):
                    gate_up(s, q)
                for s, e in downs_at(g):
                    down(s, e)

                for i, stage in enumerate((PRE_CONV0, PRE_CONV1, PRE_CONV2, PRE_CONV3)):
                    if (s := pre_at(g, stage)) is not None:
                        c, k0 = i // 2, i % 2 * 2
                        if i == 0:
                            pe.wait_ge(xnt_lo_ready, s + 1)
                            if s == 0:
                                pe.wait_ge(w_in_ready, 2)
                        elif i == 2 and s >= 1:
                            pe.wait_ge(conv_ready, HALVES * s + 1)
                        ch = slice(c * P, (c + 1) * P)
                        last = three(pre_bank(s, f"conv{c}")[:],
                                     [((tap_hi[:, k, ch], tap_lo[:, k, ch]),
                                       (xnt_hi[:, k:k + TOKENS], xnt_lo[:, k:k + TOKENS]))
                                      for k in (k0, k0 + 1)], start=(k0 == 0), stop=(k0 == 2))
                        if k0 == 2:
                            last.then_inc(conv_done, 1)
                if (s := pre_at(g, PRE_DBL)) is not None:
                    if s == 0:
                        gate_z(0)
                    pe.wait_ge(conv_ready, HALVES * (s + 1))
                    if s == 0:
                        pe.wait_ge(ld_w_x, 16)
                    for c in range(HALVES):
                        last = nc.tensor.matmul(pre_bank(s, "dbl")[0:DBL_ROWS, :], w_x_sb[:, c, :], xc[:, s % 2, c, :],
                                                start=(c == 0), stop=(c == HALVES - 1))
                    last.then_inc(dbl_done, 1)
                if (s := pre_at(g, PRE_DT)) is not None:
                    pe.wait_ge(dbl_ready, s + 1)
                    if s == 0:
                        pe.wait_ge(ld_w_dt, 16)
                    rows = slice(DT_RANK, DT_RANK + D_STATE)
                    for t in range(TILES):
                        last = nc.tensor.transpose(pre_bank(s, "c")[:, t * D_STATE:(t + 1) * D_STATE],
                                                   dbl[rows, t * P:(t + 1) * P], ident[rows, rows])
                    last.then_inc(c_turned, 1)
                    if s >= 1:
                        pe.wait_ge(c_ready, s + 1)
                    for c in range(HALVES):
                        if c == 1 and s >= 1:
                            pe.wait_ge(dt_read, 2 * s + 1)
                        nc.tensor.matmul(pre_bank(s, f"dt{c}")[:], w_dt_sb[:, c * P:(c + 1) * P],
                                         dbl[0:DT_RANK, :], start=True, stop=True).then_inc(dt_done, 1)
                if (s := pre_at(g, PRE_GATE)) is not None and s >= 1:
                    gate_z(s)

                if (s := post_at(g, POST_TURN)) is not None:
                    pe.wait_ge(summed, TILES * D_STATE * (s + 1))
                    pe.wait_ge(gz_ready, HALVES * min(s + 2, SEQS))
                    turn_four(misc_ps, acc[:, s % 2, :, 0:P]).then_inc(acc_turned, 1)
                if (s := post_at(g, POST_GATE)) is not None:
                    pe.wait_ge(y_added, HALVES * s + 1)
                    turn_four(misc_ps, acc[:, s % 2, :, P:]).then_inc(acc_turned, 1)
                    if s == 0:
                        pe.wait_ge(ld_w_out, 16)
                    pe.wait_ge(y_ready, HALVES * (s + 1))
                    for t in range(TILES):
                        for c in range(HALVES):
                            last = nc.tensor.matmul(misc_ps[:, t * D_MODEL:(t + 1) * D_MODEL],
                                                    y[:, c, t * P:(t + 1) * P], w_out_sb[:, c, :],
                                                    start=(c == 0), stop=(c == HALVES - 1))
                    last.then_inc(post_done, 1)
                if (s := post_at(g, POST_NORM)) is not None:
                    pe.wait_ge(post_read, s + 1)
                    pe.wait_ge(x2_ready, s + 1)
                    turn_four(misc_ps, x2).then_inc(x2_turned, 1)
                if (s := post_at(g, POST_LOGITS)) is not None:
                    pe.wait_ge(x2t_lo_ready, s + 1)
                    pe.wait_ge(router_split, 2)
                    four = [(v, w) for v in (x2t_hi, x2t_lo) for w in (router_hi, router_lo)]
                    for t in range(TILES):
                        for j, (v, w) in enumerate(four):
                            last = nc.tensor.matmul(misc_ps[:, t * N_EXPERTS:(t + 1) * N_EXPERTS],
                                                    v[:, s % 2, t * P:(t + 1) * P], w[:],
                                                    start=(j == 0), stop=(j == len(four) - 1))
                    last.then_inc(lg_done, 1)

        @block.scalar
        def _(act):
            def decay(m):
                s, n = divmod(m, D_STATE)
                if n == 0:
                    act.wait_ge(dt_ready, s + 1)
                if m == 0:
                    act.wait_ge(a_ready, 1)
                    act.wait_ge(zeros_ready, 3)
                if m >= DA_RING:
                    act.wait_ge(scanned, m - DA_RING + 1)
                for c in range(HALVES):
                    nc.scalar.activation(da[:, m % DA_RING, c, 1:], dt[:, c, 1:], ACT.Exp,
                                         scale=a_neg[:, c, n:n + 1]).then_inc(da_ready, 1)

            def gate_tanh(s, q):
                v = UNITS * s + q
                act.wait_ge(unit_done, v + 1)
                if v >= 2:
                    act.wait_ge(ga_ready, v - 1)
                nc.scalar.activation(th[:, v % 2, :], gate_ps[v % 2][:], ACT.Tanh, scale=0.5).then_inc(th_ready, 1)
                if on_pool(q):
                    i = pool_units(s, q)
                    if i >= 2:
                        act.wait_ge(hid_pool, i - 1)
                    nc.scalar.activation(up_cp[:, i % 2, :], up_ps[v % 2][:], ACT.Copy).then_inc(up_ready, 1)

            def move_down(s, e):
                i = FFNS * s + e
                act.wait_ge(down_done, i + 1)
                if e == 0:
                    if s >= 2:
                        act.wait_ge(out_stored[s % 2], 16 * (s // 2))
                    nc.scalar.activation(ffn_sum[:, s % 2].rearrange("p t d -> p (t d)"), down_ps[:], ACT.Copy,
                                         scale=0.5).then_inc(ffn_moved, 1)
                    return
                j = N_EXPERTS * s + e - 1
                if e == 1:
                    act.wait_ge(comb_ready, s + 1)
                if j >= 2:
                    act.wait_ge(ffn_added, j - 1)
                for t in range(TILES):
                    last = nc.scalar.activation(ffn_one[:, j % 2, t, :], down_ps[:, t * D_MODEL:(t + 1) * D_MODEL],
                                                ACT.Copy, scale=comb[:, s % 2, t, e - 1:e])
                last.then_inc(ffn_moved, 1)

            def gate_silu(s):
                for c in range(HALVES):
                    act.wait_ge(gate_done, HALVES * s + c + 1)
                    if s >= 2:
                        act.wait_ge(y_ready, HALVES * (s - 1))
                    nc.scalar.activation(gz[:, s % 2, c, :], pre_bank(s, f"gate{c}")[:], ACT.Silu).then_inc(gz_ready, 1)

            def high(dst, src):
                return nc.scalar.activation(dst, src, ACT.Copy)

            act.wait_ge(ld_w_in, 16)
            high(gate_w_hi[:], w_in_raw[:, D_INNER:]).then_inc(w_in_hi, 1)
            act.wait_ge(taps_raw, 1)
            high(tap_hi[:], tap_raw).then_inc(w_in_hi, 1)
            act.wait_ge(ld_cols, 16)
            for g in range(FIRST_SLOT, LAST_SLOT):
                if 0 <= g + LEAD < STEPS:
                    decay(g + LEAD)
                for s, q in units_at(g):
                    gate_tanh(s, q)
                for s, e in downs_at(g):
                    move_down(s, e)
                if (c := split_piece(g)) is not None:
                    act.wait_ge(ld_ffn[c * 2 // SPLIT_PIECES], 16)
                    high(pieces(ffn_hi, c), pieces(ffn_raw, c)).then_inc(ffn_w_hi, 1)

                if (s := pre_at(g, PRE_TURN)) is not None:
                    act.wait_ge(xn_turned, s + 1)
                    if s == 0:
                        act.wait_ge(zeros_ready, 3)
                    else:
                        act.wait_ge(gate_done, HALVES * s)
                    high(xnt_hi[:, PAD:], pre_bank(s, "xnt")[:]).then_inc(xnt_hi_ready, 1)
                for c in range(HALVES):
                    if (s := pre_at(g, (PRE_CONV1, PRE_CONV3)[c])) is not None:
                        act.wait_ge(conv_done, HALVES * s + c + 1)
                        if s >= 2:
                            act.wait_ge(y_added, HALVES * (s - 1))
                        nc.scalar.activation(xc[:, s % 2, c, :], pre_bank(s, f"conv{c}")[:], ACT.Silu,
                                             bias=conv_b[:, c:c + 1]).then_inc(conv_ready, 1)
                if (s := pre_at(g, PRE_DBL)) is not None:
                    if s == 0:
                        gate_silu(0)
                    act.wait_ge(dbl_done, s + 1)
                    if s >= 1:
                        act.wait_ge(b_stored, 16 * s)
                        act.wait_ge(c_turned, s)
                    nc.scalar.activation(dbl[:], pre_bank(s, "dbl")[0:DBL_ROWS, :], ACT.Copy).then_inc(dbl_ready, 1)
                    if s == 0:
                        nc.scalar.activation(a_exp[:], a_log, ACT.Exp).then_inc(a_exp_ready, 1)
                if (s := pre_at(g, PRE_DT)) is not None:
                    act.wait_ge(c_turned, s + 1)
                    if s >= 2:
                        act.wait_ge(summed, TILES * D_STATE * (s - 1))
                    nc.scalar.activation(c_tok[:, s % 2], pre_bank(s, "c")[:, 0:TILES * D_STATE]
                                         .rearrange("p (t n) -> p t n", n=D_STATE), ACT.Copy).then_inc(c_ready, 1)
                    if s >= 1:
                        act.wait_ge(dt_ready, s)
                    for c in range(HALVES):
                        act.wait_ge(dt_done, HALVES * s + c + 1)
                        nc.scalar.activation(sp_exp[:, c, :], pre_bank(s, f"dt{c}")[:], ACT.Abs,
                                             bias=b_dt[:, c:c + 1]).then_inc(sp_step, 1)
                        if s >= 1:
                            nc.scalar.activation(sp_relu[:, c, :], pre_bank(s, f"dt{c}")[:], ACT.Relu,
                                                 bias=b_dt[:, c:c + 1]).then_inc(dt_read, 1)
                    act.wait_ge(sp_step, 3 * s + 2)
                    nc.scalar.activation(sp_exp[:], sp_exp[:], ACT.Exp, scale=-1.0).then_inc(sp_step, 1)
                    act.wait_ge(sp_step, 3 * s + 3)
                    nc.scalar.activation(sp_exp[:], sp_exp[:], ACT.Ln, bias=1.0).then_inc(sp_ready, 1)
                if (s := pre_at(g, PRE_GATE)) is not None and s >= 1:
                    gate_silu(s)

                if (s := post_at(g, POST_NORM)) is not None:
                    act.wait_ge(x2_turned, s + 1)
                    if s >= 2:
                        act.wait_ge(unit_done, UNITS * (s - 1))
                    high(x2t_hi[:, s % 2, :], misc_ps[:]).then_inc(x2t_hi_ready, 1)
                if (s := post_at(g, ROUTE_A)) is not None:
                    act.wait_ge(lg_ready, s + 1)
                    nc.scalar.activation(ex[:], lg[:], ACT.Exp).then_inc(ex_ready, 1)
                if (s := post_at(g, ROUTE_B)) is not None:
                    act.wait_ge(dif_ready, s + 1)
                    nc.scalar.activation(r_exp[:], r_dif[:], ACT.Exp).then_inc(r_exp_ready, 1)

        @block.vector
        def _(dve):
            links = [0]

            def link(ins):
                links[0] += 1
                ins.then_inc(dve_link, 1)
                dve.wait_ge(dve_link, links[0])

            def stats(kind, tile):
                for t in range(TILES):
                    last = nc.vector.bn_stats(bn[kind][:, t, :], tile(t))
                link(last)
                for t in range(TILES):
                    last = nc.vector.bn_aggr(mv[kind][:, t, :], bn[kind][:, t, :])
                link(last)
                nc.vector.tensor_scalar(ve[kind][:], mv[kind][:, :, 1], EPS, None, ALU.add).then_inc(stats_ready[kind], 1)

            def normalise(kind, s, dst, tile):
                dve.wait_ge(rs_ready[kind], s + 1)
                for t in range(TILES):
                    last = nc.vector.tensor_scalar(dst[:, t, :], tile(t), mv[kind][:, t, 0:1],
                                                   rs[kind][:, t:t + 1], ALU.subtract, ALU.mult)
                return last

            def scan(m):
                dve.wait_ge(da_ready, HALVES * (m + 1))
                if m == 0:
                    dve.wait_ge(first_dbx, 1)
                else:
                    dve.wait_ge(dbx_ready, m)
                if m >= 2:
                    dve.wait_ge(turned, 2 * (m - 1))
                flat = lambda v: v.rearrange("p c t -> p (c t)")
                nc.vector.tensor_tensor_scan(flat(h[:, m % 2]), flat(da[:, m % DA_RING]), flat(dbx[:, m % DA_RING]),
                                             0.0, ALU.mult, ALU.add).then_inc(scanned, 1)

            def add_states(m):
                s, n = divmod(m, D_STATE)
                if n == 0:
                    dve.wait_ge(c_ready, s + 1)
                    if s >= 2:
                        dve.wait_ge(acc_turned, HALVES * (s - 1))
                for t in range(TILES):
                    if t % 2 == 0:
                        dve.wait_ge(turned, 2 * m + t // 2 + 1)
                    v = turn_ps[t // 2][:, (t % 2) * D_INNER:(t % 2 + 1) * D_INNER]
                    scalar = c_tok[:, s % 2, t, n:n + 1]
                    if n == 0:
                        last = nc.vector.tensor_scalar(acc[:, s % 2, t, :], v, scalar, None, ALU.mult)
                    else:
                        dve.wait_ge(summed, TILES * (m - 1) + t + 1)
                        last = nc.vector.scalar_tensor_tensor(out=acc[:, s % 2, t, :], in0=v, scalar=scalar,
                                                              in1=acc[:, s % 2, t, :], op0=ALU.mult, op1=ALU.add)
                    last.then_inc(summed, 1)

            def gate_mul(s, q):
                v = UNITS * s + q
                e, k = divmod(q, 2)
                dve.wait_ge(th_ready, v + 1)
                if v >= 2:
                    s2, q2 = divmod(v - 2, UNITS)
                    if on_pool(q2):
                        dve.wait_ge(hid_pool, pool_units(s2, q2) + 1)
                    else:
                        dve.wait_ge(hid_dve, dve_units(s2, q2) + 1)
                nc.vector.scalar_tensor_tensor(out=ga[:, v % 2, :], in0=th[:, v % 2, :], scalar=1.0,
                                               in1=gate_ps[v % 2][:], op0=ALU.add, op1=ALU.mult).then_inc(ga_ready, 1)
                if not on_pool(q):
                    dve.wait_ge(ga_ready, v + 1)
                    if FFNS * s + e >= 2:
                        dve.wait_ge(down_done, FFNS * s + e - 1)
                    nc.vector.tensor_tensor(hid[:, (FFNS * s + e) % 2, k, :], ga[:, v % 2, :], up_ps[v % 2][:],
                                            ALU.mult).then_inc(hid_dve, 1)

            def low(dst, src, hi):
                return nc.vector.tensor_tensor(dst, src, hi.bitcast(F32), ALU.subtract)

            nc.vector.memset(da[:, :, :, 0:1], 0.0).then_inc(zeros_ready, 1)
            nc.vector.memset(xnt_hi[:, 0:PAD].bitcast(F32), 0.0).then_inc(zeros_ready, 1)
            nc.vector.memset(xnt_lo[:, 0:PAD].bitcast(F32), 0.0).then_inc(zeros_ready, 1)
            for g in range(FIRST_SLOT, LAST_SLOT):
                if 0 <= g < STEPS:
                    scan(g)
                for s, q in units_at(g - 1):
                    gate_mul(s, q)
                if 1 <= g <= STEPS:
                    add_states(g - 1)
                if (c := split_piece(g)) is not None:
                    dve.wait_ge(ffn_w_hi, c + 1)
                    low(pieces(ffn_lo, c), pieces(ffn_raw, c), pieces(ffn_hi, c)).then_inc(ffn_w_ready, 1)

                if g == 1:
                    dve.wait_ge(ld_router, 16)
                    nc.vector.tensor_copy(router_hi[:], router_sb[:]).then_inc(router_split, 1)
                    dve.wait_ge(router_split, 1)
                    low(router_lo[:], router_sb[:], router_hi[:]).then_inc(router_split, 1)
                if (s := pre_at(g, PRE_STATS)) is not None:
                    dve.wait_ge(ld_x[s], 16)
                    stats("a", lambda t: x[:, s, t, :])
                    if s == 0:
                        dve.wait_ge(ld_w_in, 16)
                        dve.wait_ge(ld_conv, 16)
                        nc.vector.tensor_tensor(tap_raw, conv_raw, w_in_raw[:, 0:D_INNER]
                                                .rearrange("p (a c) -> p a c", a=1)
                                                .to_broadcast([P, D_CONV, D_INNER]), ALU.mult).then_inc(taps_raw, 1)
                if (s := pre_at(g, PRE_NORM)) is not None:
                    if s >= 1:
                        dve.wait_ge(xn_turned, s)
                    normalise("a", s, xn, lambda t: x[:, s, t, :]).then_inc(xn_ready, 1)
                if (s := pre_at(g, PRE_TURN)) is not None:
                    if s == 0:
                        dve.wait_ge(w_in_hi, 2)
                        low(gate_w_lo[:], w_in_raw[:, D_INNER:], gate_w_hi[:]).then_inc(w_in_ready, 1)
                        low(tap_lo[:], tap_raw, tap_hi[:]).then_inc(w_in_ready, 1)
                    dve.wait_ge(xnt_hi_ready, s + 1)
                    low(xnt_lo[:, PAD:], pre_bank(s, "xnt")[:], xnt_hi[:, PAD:]).then_inc(xnt_lo_ready, 1)
                if pre_at(g, PRE_DT) == 0:
                    dve.wait_ge(a_exp_ready, 1)
                    nc.vector.tensor_scalar(a_neg[:].rearrange("p c n -> p (c n)"), a_exp[:], -1.0, None,
                                            ALU.mult).then_inc(a_ready, 1)
                    for c in range(HALVES):
                        dve.wait_ge(sp_step, c + 1)
                        nc.vector.tensor_scalar(sp_relu[:, c, :], pre_bank(0, f"dt{c}")[:], b_dt[:, c:c + 1], 0.0,
                                                ALU.add, ALU.max).then_inc(dt_read, 1)
                if (s := pre_at(g, PRE_END)) is not None:
                    dve.wait_ge(sp_ready, s + 1)
                    dve.wait_ge(dt_read, HALVES * (s + 1))
                    if s >= 1:
                        dve.wait_ge(da_ready, HALVES * D_STATE * s)
                        dve.wait_ge(u_ready, s)
                    nc.vector.tensor_tensor(dt[:], sp_exp[:], sp_relu[:], ALU.add).then_inc(dt_ready, 1)
                    if s == 0:
                        dve.wait_ge(dt_ready, 1)
                        dve.wait_ge(conv_ready, HALVES)
                        nc.vector.tensor_tensor(u[:], dt[:], xc[:, 0], ALU.mult).then_inc(u_ready, 1)
                        dve.wait_ge(u_ready, 1)
                        dve.wait_ge(b_loaded[0], 16)
                        nc.vector.tensor_tensor(dbx[:, 0], u[:], b_all[:, 0:1, :].to_broadcast([P, HALVES, TOKENS]),
                                                ALU.mult).then_inc(first_dbx, 1)

                if (s := post_at(g, POST_GATE)) is not None:
                    if s >= 1:
                        dve.wait_ge(post_done, s)
                    for c in range(HALVES):
                        dve.wait_ge(acc_turned, HALVES * s + c + 1)
                        nc.vector.scalar_tensor_tensor(out=y[:, c, :], in0=xc[:, s % 2, c, :], scalar=d_par[:, c:c + 1],
                                                       in1=misc_ps[:], op0=ALU.mult, op1=ALU.add).then_inc(y_added, 1)
                if (s := post_at(g, POST_STATS)) is not None:
                    dve.wait_ge(post_done, s + 1)
                    stats("b", lambda t: misc_ps[:, t * D_MODEL:(t + 1) * D_MODEL])
                if (s := post_at(g, POST_ADD)) is not None:
                    if s >= 1:
                        dve.wait_ge(x2_turned, s)
                    normalise("b", s, x2, lambda t: misc_ps[:, t * D_MODEL:(t + 1) * D_MODEL]).then_inc(post_read, 1)
                    dve.wait_ge(post_read, s + 1)
                    nc.vector.tensor_tensor(x[:, s], x[:, s], x2[:], ALU.add).then_inc(x1_ready, 1)
                    dve.wait_ge(x1_ready, s + 1)
                    stats("c", lambda t: x[:, s, t, :])
                if (s := post_at(g, POST_NORM)) is not None:
                    normalise("c", s, x2, lambda t: x[:, s, t, :]).then_inc(x2_ready, 1)
                    dve.wait_ge(x2t_hi_ready, s + 1)
                    low(x2t_lo[:, s % 2, :], misc_ps[:], x2t_hi[:, s % 2, :]).then_inc(x2t_lo_ready, 1)
                if (s := post_at(g, ROUTE_A)) is not None:
                    dve.wait_ge(lg_done, s + 1)
                    if s == 0:
                        dve.wait_ge(ld_bias, 16)
                    wide = lambda v: v[:].rearrange("p (t a) -> p t a", a=1).to_broadcast([P, TILES, N_EXPERTS])
                    link(nc.vector.tensor_tensor(
                        lg[:], misc_ps[:, 0:TILES * N_EXPERTS].rearrange("p (t e) -> p t e", e=N_EXPERTS),
                        bias_sb[:].rearrange("p (a e) -> p a e", a=1).to_broadcast([P, TILES, N_EXPERTS]), ALU.add))
                    link(nc.vector.tensor_reduce(r_max[:], lg[:], AX_X, ALU.max))
                    nc.vector.tensor_tensor(lg[:], lg[:], wide(r_max), ALU.subtract).then_inc(lg_ready, 1)
                if (s := post_at(g, ROUTE_B)) is not None:
                    rev_wide = rev[:].rearrange("p (a e) -> p a e", a=1).to_broadcast([P, TILES, N_EXPERTS])

                    def first_of(best, key, onehot):
                        link(nc.vector.tensor_reduce(best[:], pr[:], AX_X, ALU.max))
                        link(nc.vector.tensor_tensor(eq[:], pr[:], wide(best), ALU.is_equal))
                        link(nc.vector.tensor_tensor(eq[:], eq[:], rev_wide, ALU.mult))
                        link(nc.vector.tensor_reduce(key[:], eq[:], AX_X, ALU.max))
                        link(nc.vector.tensor_tensor(onehot[:], rev_wide, wide(key), ALU.is_equal))

                    dve.wait_ge(ex_ready, s + 1)
                    dve.wait_ge(consts_ready, N_EXPERTS + 1)
                    link(nc.vector.tensor_reduce(r_sum[:], ex[:], AX_X, ALU.add))
                    link(nc.vector.reciprocal(r_inv[:], r_sum[:]))
                    link(nc.vector.tensor_tensor(pr[:], ex[:], wide(r_inv), ALU.mult))
                    first_of(m1, k1, oh1)
                    link(nc.vector.scalar_tensor_tensor(out=pr[:], in0=oh1[:], scalar=-4.0, in1=pr[:],
                                                        op0=ALU.mult, op1=ALU.add))
                    first_of(m2, k2, oh2)
                    nc.vector.tensor_tensor(r_dif[:], m2[:], m1[:], ALU.subtract).then_inc(dif_ready, 1)
                if (s := post_at(g, ROUTE_C)) is not None:
                    dve.wait_ge(r_exp_ready, s + 1)
                    link(nc.vector.tensor_scalar(r_den[:], r_exp[:], 2.0, 2.0, ALU.mult, ALU.add))
                    link(nc.vector.reciprocal(w1[:], r_den[:]))
                    link(nc.vector.tensor_tensor(w2[:], r_exp[:], w1[:], ALU.mult))
                    link(nc.vector.tensor_tensor(oh1[:], oh1[:], wide(w1), ALU.mult))
                    link(nc.vector.tensor_tensor(oh2[:], oh2[:], wide(w2), ALU.mult))
                    if s >= 2:
                        dve.wait_ge(ffn_moved, FFNS * (s - 1))
                    nc.vector.tensor_tensor(comb[:, s % 2], oh1[:], oh2[:], ALU.add).then_inc(comb_ready, 1)
                if (s := fin_at(g, FIN_STATS)) is not None:
                    dve.wait_ge(ffn_added, N_EXPERTS * (s + 1))
                    stats("f", lambda t: ffn_sum[:, s % 2, t, :])
                if (s := fin_at(g, FIN_OUT)) is not None:
                    normalise("f", s, ffn_sum[:, s % 2], lambda t: ffn_sum[:, s % 2, t, :]).then_inc(fin_scaled, 1)
                    dve.wait_ge(fin_scaled, s + 1)
                    nc.vector.tensor_tensor(ffn_sum[:, s % 2], ffn_sum[:, s % 2], x[:, s], ALU.add).then_inc(out_ready, 1)

        @block.gpsimd
        def _(pool):
            def rstd(kind, s):
                pool.wait_ge(stats_ready[kind], s + 1)
                nc.gpsimd.tensor_tensor(rs[kind][:], ve[kind][:], half_neg[:], ALU.pow).then_inc(rs_ready[kind], 1)

            def inject(m):
                s, n = divmod(m, D_STATE)
                if n == 0 or m == 1:
                    pool.wait_ge(u_ready, s + 1)
                if n % B_CHUNK == 0 or m == 1:
                    i = m // B_CHUNK
                    pool.wait_ge(b_loaded[i % 2], 16 * (i // 2 + 1))
                if m >= DA_RING:
                    pool.wait_ge(scanned, m - DA_RING + 1)
                nc.gpsimd.tensor_tensor(dbx[:, m % DA_RING], u[:],
                                        b_all[:, m % B_RING:m % B_RING + 1, :].to_broadcast([P, HALVES, TOKENS]),
                                        ALU.mult).then_inc(dbx_ready, 1)

            def add_ffn(s, e):
                pool.wait_ge(ffn_moved, FFNS * s + e + 1)
                if e >= 2:
                    pool.wait_ge(ffn_added, N_EXPERTS * s + e - 1)
                nc.gpsimd.tensor_tensor(ffn_sum[:, s % 2], ffn_sum[:, s % 2], ffn_one[:, (N_EXPERTS * s + e - 1) % 2],
                                        ALU.add).then_inc(ffn_added, 1)

            def mul_up(s, q):
                v = UNITS * s + q
                e, k = divmod(q, 2)
                pool.wait_ge(ga_ready, v + 1)
                i = pool_units(s, q)
                pool.wait_ge(up_ready, i + 1)
                if FFNS * s + e >= 2:
                    pool.wait_ge(down_done, FFNS * s + e - 1)
                nc.gpsimd.tensor_tensor(hid[:, (FFNS * s + e) % 2, k, :], ga[:, v % 2, :], up_cp[:, i % 2, :],
                                        ALU.mult).then_inc(hid_pool, 1)

            nc.gpsimd.memset(ident[:], 0.0).then_inc(ident_zero, 1)
            nc.gpsimd.memset(half_neg[:], -0.5).then_inc(consts_ready, 1)
            for e in range(N_EXPERTS):
                nc.gpsimd.memset(rev[:, e:e + 1], float(N_EXPERTS - e)).then_inc(consts_ready, 1)
            pool.wait_ge(ident_zero, 1)
            nc.gpsimd.affine_select(out=ident[:], in_=ident[:], compare_op=ALU.not_equal, fill=1.0, base=0,
                                    pattern=[[-1, P]], channel_multiplier=1).then_inc(ident_ready, 1)
            pool.wait_ge(consts_ready, N_EXPERTS + 1)
            for g in range(FIRST_SLOT, LAST_SLOT):
                if 1 <= g + LEAD < STEPS:
                    inject(g + LEAD)
                for s, q in units_at(g - 1):
                    if on_pool(q):
                        mul_up(s, q)
                for s, e in downs_at(g - 1):
                    if e >= 1:
                        add_ffn(s, e)

                if (s := pre_at(g, PRE_STATS)) is not None:
                    rstd("a", s)
                if (s := pre_at(g, PRE_END)) is not None and s >= 1:
                    pool.wait_ge(dt_ready, s + 1)
                    pool.wait_ge(conv_ready, HALVES * (s + 1))
                    pool.wait_ge(dbx_ready, D_STATE * s - 1)
                    nc.gpsimd.tensor_tensor(u[:], dt[:], xc[:, s % 2], ALU.mult).then_inc(u_ready, 1)
                if (s := post_at(g, POST_GATE)) is not None:
                    for c in range(HALVES):
                        pool.wait_ge(y_added, HALVES * s + c + 1)
                        pool.wait_ge(gz_ready, HALVES * s + c + 1)
                        nc.gpsimd.tensor_tensor(y[:, c, :], y[:, c, :], gz[:, s % 2, c, :],
                                                ALU.mult).then_inc(y_ready, 1)
                if (s := post_at(g, POST_STATS)) is not None:
                    rstd("b", s)
                if (s := post_at(g, POST_ADD)) is not None:
                    rstd("c", s)
                if (s := fin_at(g, FIN_STATS)) is not None:
                    rstd("f", s)


def kernel(**inputs):
    import numpy as np
    import concourse.bacc as bacc
    from concourse.bass_utils import run_bass_kernel_spmd

    a = {k.removeprefix("L0_"): np.asarray(v) for k, v in inputs.items()}

    w_x = a["attn_W_x"]

    def channels(v):
        return np.moveaxis(v.reshape(HALVES, P, *v.shape[1:]), 0, 1)

    def with_shared(shared, experts, axes):
        return np.ascontiguousarray(np.concatenate([shared[None], experts]).transpose(axes))

    arrays = {
        "x_in": np.ascontiguousarray(a["attn_x"].reshape(SEQS, TILES, P, D_MODEL).transpose(0, 2, 1, 3)),
        "cols": np.ascontiguousarray(np.concatenate(
            [channels(a["attn_conv_b"]), channels(a["attn_b_dt"]), channels(a["attn_D_param"]),
             channels(a["attn_A_log"]).reshape(P, HALVES * D_STATE)], axis=1)),
        "w_in": np.ascontiguousarray(a["attn_W_in"]),
        "conv_t": np.ascontiguousarray(a["attn_conv_w"].T),
        "w_x": np.ascontiguousarray(channels(np.concatenate(
            [w_x[:, :DT_RANK], w_x[:, DT_RANK + D_STATE:], w_x[:, DT_RANK:DT_RANK + D_STATE]], axis=1))),
        "w_dt": np.ascontiguousarray(a["attn_W_dt"]),
        "w_out": np.ascontiguousarray(channels(a["attn_W_out"])),
        "router_t": np.ascontiguousarray(a["ffn_router_w"].T),
        "bias_r": np.ascontiguousarray(a["ffn_expert_bias"]),
        "gate_t": with_shared(a["ffn_sw_gate"], a["ffn_ew_gate"], (2, 0, 1)),
        "up_t": with_shared(a["ffn_sw_up"], a["ffn_ew_up"], (2, 0, 1)),
        "down_t": np.ascontiguousarray(np.concatenate([a["ffn_sw_down"][None], a["ffn_ew_down"]])
                                       .reshape(FFNS, D_MODEL, 2, P).transpose(3, 0, 2, 1)),
    }
    nc = bacc.Bacc("TRN2", target_bir_lowering=False, num_devices=1)
    args = [nc.dram_tensor(k, v.shape, F32, kind="ExternalInput").ap() for k, v in arrays.items()]
    b_scratch = nc.dram_tensor("b_scratch", (SEQS, D_STATE, TOKENS), F32, kind="Internal").ap()
    out = nc.dram_tensor("out", (SEQS, P, TILES, D_MODEL), F32, kind="ExternalOutput").ap()
    build(nc, *args, b_scratch, out)
    r = run_bass_kernel_spmd(nc, [arrays], core_ids=[0])
    got = np.asarray(r.results[0]["out"])
    return np.ascontiguousarray(got.transpose(0, 2, 1, 3)).reshape(SEQS, TOKENS, D_MODEL)
```

```python
from contextlib import ExitStack

import concourse.bass as bass
from concourse import mybir

F32 = mybir.dt.float32
F32R = mybir.dt.float32r
ALU = mybir.AluOpType
ACT = mybir.ActivationFunctionType
AX_X = mybir.AxisListType.X

P = 128
SEQS, TOKENS, D_MODEL = 4, 512, 128
D_INNER, D_STATE, D_CONV, DT_RANK = 256, 16, 4, 64
DBL_ROWS = DT_RANK + 2 * D_STATE
HALVES = D_INNER // P
TILES = TOKENS // P
N_EXPERTS, D_FF = 8, 256
FFNS = N_EXPERTS + 1
PAD = D_CONV - 1
EPS = 1e-5

BLOCKS = ((0, 0, TILES), (1, 0, TILES), (2, 0, TILES), (3, 0, TILES // 2), (3, TILES // 2, TILES))
STEPS = len(BLOCKS) * D_STATE
LEAD = 2
DA_RING = LEAD + 1
B_CHUNK = 4
B_CHUNKS = D_STATE // B_CHUNK
UNITS = FFNS * 2
B_RING = 8
SPLIT_PIECES = 4
FFN_COLS = FFNS * D_FF

(PRE_STATS, PRE_NORM, PRE_TURN, PRE_CONV0, PRE_CONV1, PRE_CONV2, PRE_CONV3, PRE_DBL, PRE_DT0, PRE_DT1, PRE_SOFTPLUS,
 PRE_END, PRE_GATE0, PRE_GATE1) = range(14)
PRE_A = (6, 6, 6, 7, 8, 8, 8, 9, 9, 11, 12, 13, 12, 14)
PRE_B = (4, 5, 7, 8, 8, 9, 9, 10, 10, 11, 11, 13, 13, 14)
PRE_C = (5, 6, 7, 8, 8, 9, 9, 10, 10, 11, 11, 13, 13, 14)
PRE_SLOTS = (PRE_A, PRE_B, PRE_C, PRE_C)
SPLIT_SLOTS = (3, 7, 8, 9)
(POST_TURN0, POST_Y0, POST_TURN1, POST_Y1, POST_OUT, POST_STATS, POST_ADD, POST_NORM, POST_X2_TURN, POST_X2_LOW,
 POST_LOGITS, ROUTE, ROUTE_EXP, ROUTE_TOP, EXP_GAP, TOP_GAP, FIN_STATS, FIN_OUT) = range(18)
POST_A = (0, 1, 1, 2, 3, 3, 4, 5, 5, 6, 6, 6, 7, 10, 2, 2, 5, 6)
POST_B = (0, 1, 1, 2, 3, 3, 4, 5, 5, 6, 6, 6, 7, 10, 2, 2, 5, 6)
POST_C = (0, 1, 1, 2, 3, 3, 4, 5, 5, 6, 6, 6, 7, 10, 3, 4, 5, 7)
POST_D = (0, 1, 1, 2, 3, 3, 4, 5, 5, 6, 6, 6, 7, 10, 3, 3, 5, 7)
POST_E = (0, 1, 1, 1, 2, 3, 4, 4, 5, 6, 6, 7, 7, 11, 2, 2, 3, 8)
FFN_START = 6
UNITS_A = (1, 1, 1, 1, 0, 2, 2, 1, 1, 2, 2, 0, 2, 0, 1, 1)
UNITS_B = (1, 1, 1, 1, 0, 2, 2, 1, 1, 2, 2, 0, 2, 0, 1, 1)
UNITS_C = (0, 2, 2, 1, 1, 1, 1, 1, 2, 1, 1, 2, 0, 1, 0, 2, 0)
UNITS_D = (0, 2, 0, 2, 1, 2, 0, 2, 2, 1, 0, 1, 1, 2, 1, 1, 0)
UNITS_E = (1, 1, 1, 2, 1, 2, 2, 2, 1, 2, 2, 1, 0)
DOWNS_A = (0, 0, 0, 0, 1, 1, 1, 0, 1, 1, 0, 0, 0, 1, 0, 2, 0, 1, 0)
DOWNS_B = (0, 0, 0, 0, 1, 0, 1, 1, 1, 1, 0, 0, 0, 1, 0, 2, 0, 1, 0)
DOWNS_C = (0, 0, 0, 0, 1, 1, 1, 1, 0, 0, 1, 0, 1, 0, 1, 1, 0, 1, 0)
DOWNS_D = (0, 0, 0, 1, 0, 1, 1, 0, 1, 0, 0, 0, 1, 1, 2, 0, 0, 1)
DOWNS_E = (0, 0, 0, 1, 0, 1, 1, 1, 1, 1, 1, 1, 1)


def spread(counts):
    return [FFN_START + i for i, c in enumerate(counts) for _ in range(c)]


UNIT_SLOTS = [spread(c) for c in (UNITS_A, UNITS_B, UNITS_C, UNITS_D, UNITS_E)]
DOWN_SLOTS = [spread(c) for c in (DOWNS_A, DOWNS_B, DOWNS_C, DOWNS_D, DOWNS_E)]
ROUTE_STEPS, ROUTE_PLACES = 24, 6
POOL_A = (1, 1, 1, 0, 0, 0, 1, 0, 0, 0, 1, 1, 1, 0, 1, 1, 1, 0)
POOL_B = (1, 1, 1, 0, 0, 0, 1, 0, 0, 0, 1, 1, 1, 0, 1, 1, 1, 1)
POOL_C = (1, 1, 1, 1, 1, 0, 1, 0, 1, 1, 1, 1, 1, 0, 0, 1, 1, 1)
POOL_D = (1, 1, 1, 0, 1, 1, 1, 1, 1, 1, 0, 1, 1, 1, 1, 1, 0, 0)
POOL_E = (1, 1, 1, 1, 1, 1, 1, 0, 1, 0, 1, 0, 1, 1, 1, 1, 0, 1)
POST_SLOTS = (POST_A, POST_B, POST_C, POST_D, POST_E)
POOL_UNITS = (POOL_A, POOL_B, POOL_C, POOL_D, POOL_E)
FIRST_SLOT = PRE_A[PRE_STATS] - D_STATE
LAST_SLOT = STEPS + DOWN_SLOTS[-1][-1] + POST_E[FIN_OUT] + 1


def pre_at(g, stage):
    return next((s for s in range(SEQS) if D_STATE * (s - 1) + PRE_SLOTS[s][stage] == g), None)


def post_at(g, stage):
    return next((b for b in range(len(BLOCKS)) if D_STATE * (b + 1) + POST_SLOTS[b][stage] == g), None)


def fin_at(g, stage):
    return next((b for b in range(len(BLOCKS))
                 if D_STATE * (b + 1) + DOWN_SLOTS[b][-1] + POST_SLOTS[b][stage] == g), None)


def units_at(g):
    return [(b, q) for b in range(len(BLOCKS)) for q in range(UNITS) if D_STATE * (b + 1) + UNIT_SLOTS[b][q] == g]


def downs_at(g):
    return [(b, e) for b in range(len(BLOCKS)) for e in range(FFNS) if D_STATE * (b + 1) + DOWN_SLOTS[b][e] == g]


def tiles_of(b):
    return range(*BLOCKS[b][1:])


def tile_slice(b):
    return slice(*BLOCKS[b][1:])


def token_slice(b):
    return slice(BLOCKS[b][1] * P, BLOCKS[b][2] * P)


def tiles_before(m):
    b, n = divmod(m, D_STATE)
    return sum(D_STATE * len(tiles_of(i)) for i in range(b)) + (n * len(tiles_of(b)) if n else 0)


def turn_groups(m):
    tiles = tiles_of(m // D_STATE)
    return [(0, tiles[:2]), (1, tiles[2:])] if len(tiles) > 2 else [(m % 2, tiles)]


def groups_before(m):
    return sum(len(turn_groups(i)) for i in range(m))


def summed_from(m, bank):
    for i in reversed(range(m)):
        for k, tiles in turn_groups(i):
            if k == bank:
                return tiles_before(i) + tiles[-1] + 1 - tiles_of(i // D_STATE)[0]
    return 0


CARRIED_ON = [b for b in range(1, len(BLOCKS)) if BLOCKS[b][0] == BLOCKS[b - 1][0]]


def on_pool(b, q):
    return POOL_UNITS[b][q] == 1


def build(nc, x_in, cols, w_in, conv_t, w_x, w_dt, w_out, router_t, bias_r, gate_t, up_t, down_t,
          b_scratch, out):
    with ExitStack() as ctx:
        def sb(name, shape, dt=F32):
            return ctx.enter_context(nc.sbuf_tensor(name, shape, dt))

        def bank(name):
            return ctx.enter_context(nc.psum_tensor(name, [P, TOKENS], F32))

        def sem(name):
            return ctx.enter_context(nc.semaphore(name))

        col_sb = sb("col_sb", [P, 3 * HALVES + HALVES * D_STATE])
        conv_b = col_sb[:, 0:2]
        b_dt = col_sb[:, 2:4]
        d_par = col_sb[:, 4:6]
        a_log = col_sb[:, 6:]
        a_neg = sb("a_neg", [P, HALVES, D_STATE])
        a_exp = sb("a_exp", [P, HALVES * D_STATE])
        tap_hi = sb("tap_hi", [P, D_CONV, D_INNER], F32R)
        tap_lo = sb("tap_lo", [P, D_CONV, D_INNER], F32R)
        gate_w_hi = sb("gate_w_hi", [P, D_INNER], F32R)
        gate_w_lo = sb("gate_w_lo", [P, D_INNER], F32R)
        w_x_sb = sb("w_x_sb", [P, HALVES, DT_RANK + 2 * D_STATE])
        w_dt_sb = sb("w_dt_sb", [DT_RANK, D_INNER])
        w_out_sb = sb("w_out_sb", [P, HALVES, D_MODEL])
        router_sb = sb("router_sb", [P, N_EXPERTS])
        router_hi = sb("router_hi", [P, N_EXPERTS], F32R)
        router_lo = sb("router_lo", [P, N_EXPERTS], F32R)
        bias_sb = sb("bias_sb", [P, N_EXPERTS])
        ffn_hi = sb("ffn_hi", [P, 2, FFN_COLS], F32R)
        ffn_lo = sb("ffn_lo", [P, 2, FFN_COLS], F32R)
        down_sb = sb("down_sb", [P, FFNS, 2, D_MODEL])
        ident = sb("ident", [P, P])
        rev = sb("rev", [P, N_EXPERTS])
        half_neg = sb("half_neg", [P, TILES])

        x = sb("x", [P, SEQS, TILES, D_MODEL])
        xn = sb("xn", [P, TILES, D_MODEL])
        xnt_hi = sb("xnt_hi", [P, PAD + TOKENS], F32R)
        xnt_lo = sb("xnt_lo", [P, PAD + TOKENS], F32R)
        xc = sb("xc", [P, 2, HALVES, TOKENS])
        gz = sb("gz", [P, 2, HALVES, TOKENS])
        dbl = sb("dbl", [DBL_ROWS, TOKENS])
        c_tok = sb("c_tok", [P, 2, TILES, D_STATE])
        sp_exp = sb("sp_exp", [P, HALVES, TOKENS])
        sp_relu = sb("sp_relu", [P, HALVES, TOKENS])
        dt = sb("dt", [P, HALVES, TOKENS])
        u = sb("u", [P, HALVES, TOKENS])
        b_all = sb("b_all", [P, B_RING, TOKENS])
        da = sb("da", [P, DA_RING, HALVES, TOKENS])
        dbx = sb("dbx", [P, DA_RING, HALVES, TOKENS])
        h = sb("h", [P, 2, HALVES, TOKENS])
        carry = sb("carry", [P, D_STATE, HALVES])
        acc = sb("acc", [P, 2, TILES, D_INNER])
        y = sb("y", [P, HALVES, TOKENS])
        lg_rows = y[0:N_EXPERTS, 0, :]
        x2 = sb("x2", [P, TILES, D_MODEL])
        x2t_hi = sb("x2t_hi", [P, 2, TOKENS], F32R)
        x2t_lo = sb("x2t_lo", [P, 2, TOKENS], F32R)
        comb = sb("comb", [P, 2, TILES, N_EXPERTS])
        ffn_sum = sb("ffn_sum", [P, 2, TILES, D_MODEL])
        ffn_one = sb("ffn_one", [P, 2, TILES, D_MODEL])
        work = sb("work", [P, 10, TOKENS])
        th, up_cp, ga = (work[:, 2 * i:2 * i + 2, :] for i in range(3))
        hid = work[:, 6:10, :].rearrange("p (e k) t -> p e k t", k=2)
        flat_work = work[:].rearrange("p a t -> p (a t)")
        w_in_raw = flat_work[:, 0:2 * D_INNER]
        conv_raw = flat_work[:, 2 * D_INNER:(2 + D_CONV) * D_INNER].rearrange("p (k c) -> p k c", k=D_CONV)
        tap_raw = (flat_work[:, (2 + D_CONV) * D_INNER:(2 + 2 * D_CONV) * D_INNER]
                   .rearrange("p (k c) -> p k c", k=D_CONV))
        ffn_raw = flat_work[:, 0:2 * FFN_COLS]

        bn = {k: sb(f"bn_{k}", [P, TILES, 6]) for k in "abcf"}
        mv = {k: sb(f"mv_{k}", [P, TILES, 2]) for k in "abcf"}
        ve = {k: sb(f"ve_{k}", [P, TILES]) for k in "abcf"}
        rs = {k: sb(f"rs_{k}", [P, TILES]) for k in "abcf"}
        minus_mean = {k: sb(f"minus_mean_{k}", [P, TILES]) for k in "af"}
        shift = {k: sb(f"shift_{k}", [P, TILES]) for k in "af"}
        lg = sb("lg", [P, TILES, N_EXPERTS])
        ex = sb("ex", [P, TILES, N_EXPERTS])
        pr = sb("pr", [P, TILES, N_EXPERTS])
        eq = sb("eq", [P, TILES, N_EXPERTS])
        oh1 = sb("oh1", [P, TILES, N_EXPERTS])
        oh2 = sb("oh2", [P, TILES, N_EXPERTS])
        r_max = sb("r_max", [P, TILES])
        r_sum = sb("r_sum", [P, TILES])
        r_inv = sb("r_inv", [P, TILES])
        m1 = sb("m1", [P, TILES])
        m2 = sb("m2", [P, TILES])
        k1 = sb("k1", [P, TILES])
        k2 = sb("k2", [P, TILES])
        r_dif = sb("r_dif", [P, TILES])
        r_exp = sb("r_exp", [P, TILES])
        r_den = sb("r_den", [P, TILES])
        w1 = sb("w1", [P, TILES])
        w2 = sb("w2", [P, TILES])

        gate_ps = [bank("gate_ps0"), bank("gate_ps1")]
        up_ps = [bank("up_ps0"), bank("up_ps1")]
        down_ps = bank("down_ps")
        turn_ps = [bank("turn_ps0"), bank("turn_ps1")]
        misc_ps = bank("misc_ps")
        PRE_BANKS = {"xnt": misc_ps, "conv0": gate_ps[0], "conv1": up_ps[0], "gate0": gate_ps[1],
                     "gate1": up_ps[1], "dbl": turn_ps[0], "c": turn_ps[1], "dt0": down_ps, "dt1": misc_ps}

        def pre_bank(s, name):
            return PRE_BANKS[name] if s == 0 else misc_ps

        ld_x = [sem(f"ld_x{s}") for s in range(SEQS)]
        ld_cols = sem("ld_cols")
        ld_conv = sem("ld_conv")
        ld_w_in = sem("ld_w_in")
        ld_w_x = sem("ld_w_x")
        ld_w_dt = sem("ld_w_dt")
        ld_w_out = sem("ld_w_out")
        ld_router = sem("ld_router")
        ld_bias = sem("ld_bias")
        ld_ffn = [sem("ld_gate_w"), sem("ld_up_w")]
        ld_down = sem("ld_down")
        b_stored = sem("b_stored")
        b_loaded = [sem(f"b_loaded{c}") for c in range(2)]
        out_stored = [sem(f"out_stored{i}") for i in range(2)]

        ident_zero = sem("ident_zero")
        ident_ready = sem("ident_ready")
        consts_ready = sem("consts_ready")
        rs_ready = {k: sem(f"rs_ready_{k}") for k in "abcf"}
        shift_ready = {k: sem(f"shift_ready_{k}") for k in "af"}
        u_ready = sem("u_ready")
        dbx_ready = sem("dbx_ready")
        y_ready = sem("y_ready")
        ffn_added = sem("ffn_added")
        hid_pool = sem("hid_pool")
        zeros_ready = sem("zeros_ready")
        w_in_hi = sem("w_in_hi")
        taps_raw = sem("taps_raw")
        w_in_ready = sem("w_in_ready")
        router_split = sem("router_split")
        ffn_w_ready = sem("ffn_w_ready")
        xnt_lo_ready = sem("xnt_lo_ready")
        x2t_lo_ready = sem("x2t_lo_ready")
        a_ready = sem("a_ready")
        dve_link = sem("dve_link")
        stats_ready = {k: sem(f"stats_ready_{k}") for k in "abcf"}
        xn_ready = sem("xn_ready")
        dt_ready = sem("dt_ready")
        first_dbx = sem("first_dbx")
        scanned = sem("scanned")
        summed = sem("summed")
        y_added = sem("y_added")
        post_read = sem("post_read")
        x1_ready = sem("x1_ready")
        x2_ready = sem("x2_ready")
        routed = sem("routed")
        ga_ready = sem("ga_ready")
        hid_dve = sem("hid_dve")
        fin_scaled = sem("fin_scaled")
        out_ready = sem("out_ready")
        a_exp_ready = sem("a_exp_ready")
        xnt_hi_ready = sem("xnt_hi_ready")
        ffn_w_hi = sem("ffn_w_hi")
        conv_ready = sem("conv_ready")
        gz_ready = sem("gz_ready")
        dbl_ready = sem("dbl_ready")
        c_ready = sem("c_ready")
        dt_read = sem("dt_read")
        sp_step = sem("sp_step")
        sp_ready = sem("sp_ready")
        da_ready = sem("da_ready")
        x2t_hi_ready = sem("x2t_hi_ready")
        carried = sem("carried")
        lg_moved = sem("lg_moved")
        ex_ready = sem("ex_ready")
        r_exp_ready = sem("r_exp_ready")
        ffn_moved = sem("ffn_moved")
        th_ready = sem("th_ready")
        up_ready = sem("up_ready")
        xn_turned = sem("xn_turned")
        conv_done = sem("conv_done")
        gate_done = sem("gate_done")
        dbl_done = sem("dbl_done")
        c_turned = sem("c_turned")
        dt_done = sem("dt_done")
        turned = sem("turned")
        acc_turned = sem("acc_turned")
        post_done = sem("post_done")
        x2_turned = sem("x2_turned")
        lg_product = sem("lg_product")
        lg_done = sem("lg_done")
        unit_done = sem("unit_done")
        down_done = sem("down_done")

        def pool_units(b, q):
            return sum(map(sum, POOL_UNITS[:b])) + sum(POOL_UNITS[b][:q])

        def dve_units(b, q):
            return b * UNITS + q - pool_units(b, q)

        def by_scalar(kind, i):
            return i >= 1 if kind == "a" else kind == "f" and i < len(BLOCKS) - 1

        def split_piece(g):
            return SPLIT_SLOTS.index(g) if g in SPLIT_SLOTS else None

        def pieces(tile, c):
            size = 2 * FFN_COLS // SPLIT_PIECES
            flat = tile if tile is ffn_raw else tile[:].rearrange("p a c -> p (a c)")
            return flat[:, c * size:(c + 1) * size]

        block = ctx.enter_context(nc.Block())

        @block.sync
        def _(sp):
            def load_b(b, c):
                s = BLOCKS[b][0]
                i = B_CHUNKS * b + c
                if i >= 2:
                    sp.wait_ge(dbx_ready, B_CHUNK * (i - 1) - 1)
                r = B_CHUNK * (i % 2)
                sp.dma_start(b_all[:, r:r + B_CHUNK, :],
                             b_scratch[s, B_CHUNK * c:B_CHUNK * (c + 1)].rearrange("(a n) t -> a n t", a=1)
                             .to_broadcast([P, B_CHUNK, TOKENS])).then_inc(b_loaded[i % 2], 16)

            def store(b):
                sp.wait_ge(out_ready, b + 1)
                sp.dma_start(out[BLOCKS[b][0]][:, tile_slice(b)],
                             ffn_sum[:, b % 2, tile_slice(b)]).then_inc(out_stored[b % 2], 16)

            sp.dma_start(x[:, 0], x_in[0]).then_inc(ld_x[0], 16)
            sp.dma_start(w_in_raw, w_in).then_inc(ld_w_in, 16)
            sp.dma_start(conv_raw, conv_t.rearrange("(a k) c -> a k c", a=1)
                         .to_broadcast([P, D_CONV, D_INNER])).then_inc(ld_conv, 16)
            sp.dma_start(col_sb[:], cols).then_inc(ld_cols, 16)
            sp.dma_start(w_x_sb[:], w_x).then_inc(ld_w_x, 16)
            sp.dma_start(w_dt_sb[:], w_dt).then_inc(ld_w_dt, 16)
            for g in range(FIRST_SLOT, LAST_SLOT):
                if (s := pre_at(g, PRE_DBL)) is not None:
                    sp.wait_ge(dbl_ready, s + 1)
                    sp.dma_start(b_scratch[s], dbl[DT_RANK + D_STATE:, :]).then_inc(b_stored, 16)
                    if s == 0:
                        sp.wait_ge(b_stored, 16)
                        load_b(0, 0)
                        load_b(0, 1)
                for c in range(B_CHUNKS):
                    b, r = divmod(g + LEAD - B_CHUNK * (c - 1), D_STATE)
                    if r == 0 and 0 <= b < len(BLOCKS) and B_CHUNKS * b + c >= 2:
                        if c == 0 and b not in CARRIED_ON:
                            sp.wait_ge(b_stored, 16 * (BLOCKS[b][0] + 1))
                        load_b(b, c)
                if pre_at(g, PRE_DBL) == 0:
                    sp.dma_start(x[:, 1], x_in[1]).then_inc(ld_x[1], 16)
                    sp.dma_start(w_out_sb[:], w_out).then_inc(ld_w_out, 16)
                    sp.dma_start(router_sb[:], router_t).then_inc(ld_router, 16)
                    sp.dma_start(bias_sb[:], bias_r.rearrange("(a e) -> a e", a=1)
                                 .to_broadcast([P, N_EXPERTS])).then_inc(ld_bias, 16)
                    sp.wait_ge(w_in_ready, 2)
                    for i in range(2):
                        sp.dma_start(ffn_raw[:, i * FFN_COLS:(i + 1) * FFN_COLS],
                                     (gate_t, up_t)[i].rearrange("d e f -> d (e f)")).then_inc(ld_ffn[i], 16)
                    sp.dma_start(down_sb[:], down_t).then_inc(ld_down, 16)
                    for i in range(2, SEQS):
                        sp.dma_start(x[:, i], x_in[i]).then_inc(ld_x[i], 16)
                if (b := fin_at(g, FIN_OUT)) is not None:
                    store(b)
            for i in range(2):
                sp.wait_ge(out_stored[i], 16 * len(BLOCKS[i::2]))

        @block.tensor
        def _(pe):
            def turn_states(m):
                pe.wait_ge(scanned, m + 1)
                for bank, tiles in turn_groups(m):
                    if summed_from(m, bank):
                        pe.wait_ge(summed, summed_from(m, bank))
                    for i, t in enumerate(tiles):
                        for c in range(HALVES):
                            last = nc.tensor.transpose(turn_ps[bank][:, i * D_INNER + c * P:i * D_INNER + (c + 1) * P],
                                                       h[:, m % 2, c, t * P:(t + 1) * P], ident[:])
                    last.then_inc(turned, 1)

            def three(dst, pairs, start=True, stop=True):
                for i, ((w_hi, w_lo), (v_hi, v_lo)) in enumerate(pairs):
                    for j, (w, v) in enumerate(((w_hi, v_hi), (w_hi, v_lo), (w_lo, v_hi))):
                        last = nc.tensor.matmul(dst, w, v, start=(start and i == 0 and j == 0),
                                                stop=(stop and i == len(pairs) - 1 and j == 2))
                return last

            def gate_up(b, q):
                e, k = divmod(q, 2)
                v = UNITS * b + q
                if v == 0:
                    pe.wait_ge(ffn_w_ready, SPLIT_PIECES)
                if q == 0:
                    pe.wait_ge(x2t_lo_ready, b + 1)
                if v >= 2:
                    pe.wait_ge(ga_ready, v - 1)
                    b2, q2 = divmod(v - 2, UNITS)
                    if on_pool(b2, q2):
                        pe.wait_ge(up_ready, pool_units(b2, q2) + 1)
                    else:
                        pe.wait_ge(hid_dve, dve_units(b2, q2) + 1)
                sl = token_slice(b)
                x2t_both = (x2t_hi[:, b % 2, sl], x2t_lo[:, b % 2, sl])
                col = e * D_FF + k * P
                for i, ps in enumerate((gate_ps, up_ps)):
                    last = three(ps[v % 2][:, sl], [((ffn_hi[:, i, col:col + P], ffn_lo[:, i, col:col + P]), x2t_both)])
                last.then_inc(unit_done, 1)

            def down(b, e):
                for k in range(2):
                    q = 2 * e + k
                    if on_pool(b, q):
                        pe.wait_ge(hid_pool, pool_units(b, q) + 1)
                    else:
                        pe.wait_ge(hid_dve, dve_units(b, q) + 1)
                i = FFNS * b + e
                if i == 0:
                    pe.wait_ge(ld_down, 16)
                else:
                    pe.wait_ge(ffn_moved, i)
                for t in tiles_of(b):
                    for k in range(2):
                        last = nc.tensor.matmul(down_ps[:, t * D_MODEL:(t + 1) * D_MODEL],
                                                hid[:, i % 2, k, t * P:(t + 1) * P], down_sb[:, e, k, :],
                                                start=(k == 0), stop=(k == 1))
                last.then_inc(down_done, 1)

            def turn_tiles(dst, src, tiles):
                for t in tiles:
                    last = nc.tensor.transpose(dst[:, t * P:(t + 1) * P], src[:, t, :], ident[:])
                return last

            def gate_z(s, c):
                if s >= 1:
                    if c == 0:
                        pe.wait_ge(dt_read, HALVES * (s + 1))
                    else:
                        pe.wait_ge(gz_ready, HALVES * s + 1)
                ch = slice(c * P, (c + 1) * P)
                three(pre_bank(s, f"gate{c}")[:],
                      [((gate_w_hi[:, ch], gate_w_lo[:, ch]), (xnt_hi[:, PAD:], xnt_lo[:, PAD:]))]
                      ).then_inc(gate_done, 1)

            for g in range(FIRST_SLOT, LAST_SLOT):
                if 1 <= g <= STEPS:
                    turn_states(g - 1)
                if (s := pre_at(g, PRE_TURN)) is not None:
                    pe.wait_ge(xn_ready, s + 1)
                    if s == 0:
                        pe.wait_ge(ident_ready, 1)
                    elif s == 1:
                        pe.wait_ge(dt_read, HALVES)
                    else:
                        pe.wait_ge(routed, ROUTE_STEPS * (s - 2) + 1)
                    turn_tiles(pre_bank(s, "xnt"), xn, range(TILES)).then_inc(xn_turned, 1)
                if (b := post_at(g, POST_LOGITS)) is not None:
                    pe.wait_ge(x2t_lo_ready, b + 1)
                    pe.wait_ge(router_split, 2)
                    four = [(w, v) for w in (router_hi, router_lo) for v in (x2t_hi, x2t_lo)]
                    for j, (w, v) in enumerate(four):
                        last = nc.tensor.matmul(misc_ps[0:N_EXPERTS, token_slice(b)], w[:], v[:, b % 2, token_slice(b)],
                                                start=(j == 0), stop=(j == len(four) - 1))
                    last.then_inc(lg_product, 1)
                for b, q in units_at(g):
                    gate_up(b, q)
                for b, e in downs_at(g):
                    down(b, e)

                for i, stage in enumerate((PRE_CONV0, PRE_CONV1, PRE_CONV2, PRE_CONV3)):
                    if (s := pre_at(g, stage)) is not None:
                        c, k0 = i // 2, i % 2 * 2
                        if i == 0:
                            pe.wait_ge(xnt_lo_ready, s + 1)
                            if s == 0:
                                pe.wait_ge(w_in_ready, 2)
                        elif i == 2 and s >= 1:
                            pe.wait_ge(conv_ready, HALVES * s + 1)
                        ch = slice(c * P, (c + 1) * P)
                        last = three(pre_bank(s, f"conv{c}")[:],
                                     [((tap_hi[:, k, ch], tap_lo[:, k, ch]),
                                       (xnt_hi[:, k:k + TOKENS], xnt_lo[:, k:k + TOKENS]))
                                      for k in (k0, k0 + 1)], start=(k0 == 0), stop=(k0 == 2))
                        if k0 == 2:
                            last.then_inc(conv_done, 1)
                if (s := pre_at(g, PRE_DBL)) is not None:
                    if s == 0:
                        for c in range(HALVES):
                            gate_z(0, c)
                    pe.wait_ge(conv_ready, HALVES * (s + 1))
                    if s == 0:
                        pe.wait_ge(ld_w_x, 16)
                    for c in range(HALVES):
                        last = nc.tensor.matmul(pre_bank(s, "dbl")[0:DBL_ROWS, :], w_x_sb[:, c, :], xc[:, s % 2, c, :],
                                                start=(c == 0), stop=(c == HALVES - 1))
                    last.then_inc(dbl_done, 1)
                if (s := pre_at(g, PRE_DT0)) is not None:
                    pe.wait_ge(dbl_ready, s + 1)
                    rows = slice(DT_RANK, DT_RANK + D_STATE)
                    for t in range(TILES):
                        last = nc.tensor.transpose(pre_bank(s, "c")[:, t * D_STATE:(t + 1) * D_STATE],
                                                   dbl[rows, t * P:(t + 1) * P], ident[rows, rows])
                    last.then_inc(c_turned, 1)
                    if s == 0:
                        pe.wait_ge(ld_w_dt, 16)
                for c in range(HALVES):
                    if (s := pre_at(g, (PRE_DT0, PRE_DT1)[c])) is not None:
                        if s >= 1:
                            if c == 0:
                                pe.wait_ge(c_ready, s + 1)
                            else:
                                pe.wait_ge(dt_read, HALVES * s + 1)
                        nc.tensor.matmul(pre_bank(s, f"dt{c}")[:], w_dt_sb[:, c * P:(c + 1) * P],
                                         dbl[0:DT_RANK, :], start=True, stop=True).then_inc(dt_done, 1)
                for c in range(HALVES):
                    if (s := pre_at(g, (PRE_GATE0, PRE_GATE1)[c])) is not None and s >= 1:
                        gate_z(s, c)

                if (b := post_at(g, POST_TURN0)) is not None:
                    pe.wait_ge(summed, tiles_before(D_STATE * (b + 1)))
                    pe.wait_ge(gz_ready, HALVES * min(b + 2, SEQS))
                    turn_tiles(misc_ps, acc[:, BLOCKS[b][0] % 2, :, 0:P], tiles_of(b)).then_inc(acc_turned, 1)
                if (b := post_at(g, POST_TURN1)) is not None:
                    pe.wait_ge(y_added, HALVES * b + 1)
                    turn_tiles(misc_ps, acc[:, BLOCKS[b][0] % 2, :, P:], tiles_of(b)).then_inc(acc_turned, 1)
                if (b := post_at(g, POST_OUT)) is not None:
                    if b == 0:
                        pe.wait_ge(ld_w_out, 16)
                    pe.wait_ge(y_ready, HALVES * (b + 1))
                    for t in tiles_of(b):
                        for c in range(HALVES):
                            last = nc.tensor.matmul(misc_ps[:, t * D_MODEL:(t + 1) * D_MODEL],
                                                    y[:, c, t * P:(t + 1) * P], w_out_sb[:, c, :],
                                                    start=(c == 0), stop=(c == HALVES - 1))
                    last.then_inc(post_done, 1)
                if (b := post_at(g, POST_X2_TURN)) is not None:
                    pe.wait_ge(post_read, b + 1)
                    pe.wait_ge(x2_ready, b + 1)
                    turn_tiles(misc_ps, x2, tiles_of(b)).then_inc(x2_turned, 1)
                if (b := post_at(g, POST_LOGITS)) is not None:
                    pe.wait_ge(lg_moved, b + 1)
                    for t in tiles_of(b):
                        last = nc.tensor.transpose(misc_ps[:, t * N_EXPERTS:(t + 1) * N_EXPERTS],
                                                   lg_rows[:, t * P:(t + 1) * P], ident[0:N_EXPERTS, 0:N_EXPERTS])
                    last.then_inc(lg_done, 1)

        @block.scalar
        def _(act):
            def decay(m):
                b, n = divmod(m, D_STATE)
                s = BLOCKS[b][0]
                if n == 0:
                    act.wait_ge(dt_ready, s + 1)
                if m == 0:
                    act.wait_ge(a_ready, 1)
                    act.wait_ge(zeros_ready, 3)
                if m >= DA_RING:
                    act.wait_ge(scanned, m - DA_RING + 1)
                sl = slice(max(1, token_slice(b).start), token_slice(b).stop)
                for c in range(HALVES):
                    nc.scalar.activation(da[:, m % DA_RING, c, sl], dt[:, c, sl], ACT.Exp,
                                         scale=a_neg[:, c, n:n + 1]).then_inc(da_ready, 1)

            def carry_states(m):
                act.wait_ge(scanned, m + 1)
                last = token_slice(m // D_STATE).stop - 1
                nc.scalar.activation(carry[:, m % D_STATE, :], h[:, m % 2, :, last], ACT.Copy).then_inc(carried, 1)

            def start_sums(m):
                b = m // D_STATE
                s = BLOCKS[b][0]
                if s >= 2:
                    act.wait_ge(acc_turned, HALVES * (s - 1))
                act.wait_ge(c_ready, s + 1)
                if m >= 1:
                    act.wait_ge(summed, tiles_before(m))
                for k, (bank, tiles) in enumerate(turn_groups(m)):
                    act.wait_ge(turned, groups_before(m) + k + 1)
                    for i, t in enumerate(tiles):
                        nc.scalar.activation(acc[:, s % 2, t, :], turn_ps[bank][:, i * D_INNER:(i + 1) * D_INNER],
                                             ACT.Copy, scale=c_tok[:, s % 2, t, 0:1]).then_inc(summed, 1)

            def normalise(kind, i, tiles, dst, tile):
                if not by_scalar(kind, i):
                    return
                act.wait_ge(shift_ready[kind], i if kind == "a" else i + 1)
                for t in tiles:
                    last = nc.scalar.activation(dst[:, t, :], tile(t), ACT.Identity, bias=shift[kind][:, t:t + 1],
                                                scale=rs[kind][:, t:t + 1])
                last.then_inc({"a": xn_ready, "f": fin_scaled}[kind], 1)

            def gate_tanh(b, q):
                v = UNITS * b + q
                sl = token_slice(b)
                act.wait_ge(unit_done, v + 1)
                if v >= 2:
                    act.wait_ge(ga_ready, v - 1)
                nc.scalar.activation(th[:, v % 2, sl], gate_ps[v % 2][:, sl], ACT.Tanh, scale=0.5).then_inc(th_ready, 1)
                if on_pool(b, q):
                    i = pool_units(b, q)
                    if i >= 2:
                        act.wait_ge(hid_pool, i - 1)
                    nc.scalar.activation(up_cp[:, i % 2, sl], up_ps[v % 2][:, sl], ACT.Copy).then_inc(up_ready, 1)

            def move_down(b, e):
                i = FFNS * b + e
                act.wait_ge(down_done, i + 1)
                if e == 0:
                    if b >= 2:
                        act.wait_ge(out_stored[b % 2], 16 * (b // 2))
                    nc.scalar.activation(ffn_sum[:, b % 2, tile_slice(b)].rearrange("p t d -> p (t d)"),
                                         down_ps[:, token_slice(b)], ACT.Copy, scale=0.5).then_inc(ffn_moved, 1)
                    return
                j = N_EXPERTS * b + e - 1
                if e == 1:
                    act.wait_ge(routed, ROUTE_STEPS * (b + 1))
                if j >= 2:
                    act.wait_ge(ffn_added, j - 1)
                for t in tiles_of(b):
                    last = nc.scalar.activation(ffn_one[:, j % 2, t, :], down_ps[:, t * D_MODEL:(t + 1) * D_MODEL],
                                                ACT.Copy, scale=comb[:, b % 2, t, e - 1:e])
                last.then_inc(ffn_moved, 1)

            def gate_silu(s, c):
                act.wait_ge(gate_done, HALVES * s + c + 1)
                if s >= 2:
                    act.wait_ge(y_ready, HALVES * (s - 1))
                nc.scalar.activation(gz[:, s % 2, c, :], pre_bank(s, f"gate{c}")[:], ACT.Silu).then_inc(gz_ready, 1)

            def high(dst, src):
                return nc.scalar.activation(dst, src, ACT.Copy)

            act.wait_ge(ld_w_in, 16)
            high(gate_w_hi[:], w_in_raw[:, D_INNER:]).then_inc(w_in_hi, 1)
            act.wait_ge(taps_raw, 1)
            high(tap_hi[:], tap_raw).then_inc(w_in_hi, 1)
            act.wait_ge(ld_cols, 16)
            for g in range(FIRST_SLOT, LAST_SLOT):
                if 0 <= g + LEAD < STEPS:
                    decay(g + LEAD)
                if (b := post_at(g, ROUTE_EXP)) is not None:
                    act.wait_ge(routed, ROUTE_STEPS * b + 3)
                    nc.scalar.activation(ex[:, tile_slice(b)], lg[:, tile_slice(b)], ACT.Exp).then_inc(ex_ready, 1)
                if (b := post_at(g, ROUTE_TOP)) is not None:
                    act.wait_ge(routed, ROUTE_STEPS * b + 18)
                    nc.scalar.activation(r_exp[:, tile_slice(b)], r_dif[:, tile_slice(b)],
                                         ACT.Exp).then_inc(r_exp_ready, 1)
                if (s := pre_at(g, PRE_NORM)) is not None:
                    if s >= 1:
                        act.wait_ge(xn_turned, s)
                    normalise("a", s, range(TILES), xn, lambda t: x[:, s, t, :])
                if (b := fin_at(g, FIN_OUT)) is not None:
                    normalise("f", b, tiles_of(b), ffn_sum[:, b % 2], lambda t: ffn_sum[:, b % 2, t, :])
                if 1 <= g <= STEPS and (g - 1) % D_STATE == 0:
                    start_sums(g - 1)
                if g - 1 >= 0 and (g - 1) // D_STATE + 1 in CARRIED_ON:
                    carry_states(g - 1)
                if (b := post_at(g, POST_LOGITS)) is not None:
                    act.wait_ge(lg_product, b + 1)
                    act.wait_ge(post_done, b + 1)
                    nc.scalar.activation(lg_rows[:, token_slice(b)], misc_ps[0:N_EXPERTS, token_slice(b)],
                                         ACT.Copy).then_inc(lg_moved, 1)
                for b, q in units_at(g):
                    gate_tanh(b, q)
                for b, e in downs_at(g):
                    move_down(b, e)
                if (c := split_piece(g)) is not None:
                    act.wait_ge(ld_ffn[c * 2 // SPLIT_PIECES], 16)
                    high(pieces(ffn_hi, c), pieces(ffn_raw, c)).then_inc(ffn_w_hi, 1)

                if (s := pre_at(g, PRE_TURN)) is not None:
                    act.wait_ge(xn_turned, s + 1)
                    if s == 0:
                        act.wait_ge(zeros_ready, 3)
                    else:
                        act.wait_ge(gate_done, HALVES * s)
                    high(xnt_hi[:, PAD:], pre_bank(s, "xnt")[:]).then_inc(xnt_hi_ready, 1)
                for c in range(HALVES):
                    if (s := pre_at(g, (PRE_CONV1, PRE_CONV3)[c])) is not None:
                        act.wait_ge(conv_done, HALVES * s + c + 1)
                        if s >= 2:
                            act.wait_ge(y_added, HALVES * (s - 1))
                        nc.scalar.activation(xc[:, s % 2, c, :], pre_bank(s, f"conv{c}")[:], ACT.Silu,
                                             bias=conv_b[:, c:c + 1]).then_inc(conv_ready, 1)
                if (s := pre_at(g, PRE_DBL)) is not None:
                    if s == 0:
                        for c in range(HALVES):
                            gate_silu(0, c)
                    act.wait_ge(dbl_done, s + 1)
                    if s >= 1:
                        act.wait_ge(b_stored, 16 * s)
                        act.wait_ge(c_turned, s)
                    nc.scalar.activation(dbl[:], pre_bank(s, "dbl")[0:DBL_ROWS, :], ACT.Copy).then_inc(dbl_ready, 1)
                    if s == 0:
                        nc.scalar.activation(a_exp[:], a_log, ACT.Exp).then_inc(a_exp_ready, 1)
                if (s := pre_at(g, PRE_DT0)) is not None:
                    act.wait_ge(c_turned, s + 1)
                    if s >= 2:
                        act.wait_ge(summed, TILES * D_STATE * (s - 1))
                    nc.scalar.activation(c_tok[:, s % 2], pre_bank(s, "c")[:, 0:TILES * D_STATE]
                                         .rearrange("p (t n) -> p t n", n=D_STATE), ACT.Copy).then_inc(c_ready, 1)
                for c in range(HALVES):
                    if (s := pre_at(g, (PRE_DT0, PRE_DT1)[c])) is not None:
                        if c == 0 and s >= 1:
                            act.wait_ge(dt_ready, s)
                        act.wait_ge(dt_done, HALVES * s + c + 1)
                        nc.scalar.activation(sp_exp[:, c, :], pre_bank(s, f"dt{c}")[:], ACT.Abs,
                                             bias=b_dt[:, c:c + 1]).then_inc(sp_step, 1)
                        if s >= 1:
                            nc.scalar.activation(sp_relu[:, c, :], pre_bank(s, f"dt{c}")[:], ACT.Relu,
                                                 bias=b_dt[:, c:c + 1]).then_inc(dt_read, 1)
                if (s := pre_at(g, PRE_SOFTPLUS)) is not None:
                    act.wait_ge(sp_step, 3 * s + 2)
                    nc.scalar.activation(sp_exp[:], sp_exp[:], ACT.Exp, scale=-1.0).then_inc(sp_step, 1)
                    act.wait_ge(sp_step, 3 * s + 3)
                    nc.scalar.activation(sp_exp[:], sp_exp[:], ACT.Ln, bias=1.0).then_inc(sp_ready, 1)
                for c in range(HALVES):
                    if (s := pre_at(g, (PRE_GATE0, PRE_GATE1)[c])) is not None and s >= 1:
                        gate_silu(s, c)

                if (b := post_at(g, POST_X2_TURN)) is not None:
                    act.wait_ge(x2_turned, b + 1)
                    if b >= 2:
                        act.wait_ge(unit_done, UNITS * (b - 1))
                    high(x2t_hi[:, b % 2, token_slice(b)], misc_ps[:, token_slice(b)]).then_inc(x2t_hi_ready, 1)

        @block.vector
        def _(dve):
            links = [0]

            def link(ins):
                links[0] += 1
                ins.then_inc(dve_link, 1)
                dve.wait_ge(dve_link, links[0])

            def stats(kind, i, tiles, tile):
                for t in tiles:
                    last = nc.vector.bn_stats(bn[kind][:, t, :], tile(t))
                link(last)
                for t in tiles:
                    last = nc.vector.bn_aggr(mv[kind][:, t, :], bn[kind][:, t, :])
                link(last)
                tl = slice(tiles[0], tiles[-1] + 1)
                if by_scalar(kind, i):
                    nc.vector.tensor_scalar(minus_mean[kind][:, tl], mv[kind][:, tl, 0], -1.0, None, ALU.mult)
                nc.vector.tensor_scalar(ve[kind][:, tl], mv[kind][:, tl, 1], EPS, None,
                                        ALU.add).then_inc(stats_ready[kind], 1)

            def normalise(kind, i, tiles, dst, tile):
                dve.wait_ge(rs_ready[kind], i + 1)
                for t in tiles:
                    last = nc.vector.tensor_scalar(dst[:, t, :], tile(t), mv[kind][:, t, 0:1],
                                                   rs[kind][:, t:t + 1], ALU.subtract, ALU.mult)
                return last

            def scan(m):
                b, n = divmod(m, D_STATE)
                dve.wait_ge(da_ready, HALVES * (m + 1))
                if m == 0:
                    dve.wait_ge(first_dbx, 1)
                else:
                    dve.wait_ge(dbx_ready, m)
                if m >= 2:
                    dve.wait_ge(turned, groups_before(m - 1))
                    if (m - 2) // D_STATE + 1 in CARRIED_ON:
                        dve.wait_ge(carried, m - 1 - D_STATE * (CARRIED_ON[0] - 1))
                if len(tiles_of(b)) == TILES:
                    flat = lambda v: v.rearrange("p c t -> p (c t)")
                    nc.vector.tensor_tensor_scan(flat(h[:, m % 2]), flat(da[:, m % DA_RING]), flat(dbx[:, m % DA_RING]),
                                                 0.0, ALU.mult, ALU.add).then_inc(scanned, 1)
                    return
                if b in CARRIED_ON:
                    dve.wait_ge(carried, D_STATE * (b - CARRIED_ON[0]) + n + 1)
                sl = token_slice(b)
                for c in range(HALVES):
                    last = nc.vector.tensor_tensor_scan(h[:, m % 2, c, sl], da[:, m % DA_RING, c, sl],
                                                        dbx[:, m % DA_RING, c, sl],
                                                        carry[:, n, c:c + 1] if b in CARRIED_ON else 0.0,
                                                        ALU.mult, ALU.add)
                last.then_inc(scanned, 1)

            def add_states(m, k):
                b, n = divmod(m, D_STATE)
                if n == 0 or k >= len(turn_groups(m)):
                    return
                s = BLOCKS[b][0]
                bank, tiles = turn_groups(m)[k]
                dve.wait_ge(turned, groups_before(m) + k + 1)
                for i, t in enumerate(tiles):
                    dve.wait_ge(summed, tiles_before(m) if n == 1 else tiles_before(m - 1) + t - tiles_of(b)[0] + 1)
                    nc.vector.scalar_tensor_tensor(out=acc[:, s % 2, t, :],
                                                   in0=turn_ps[bank][:, i * D_INNER:(i + 1) * D_INNER],
                                                   scalar=c_tok[:, s % 2, t, n:n + 1], in1=acc[:, s % 2, t, :],
                                                   op0=ALU.mult, op1=ALU.add).then_inc(summed, 1)

            def gate_mul(b, q):
                v = UNITS * b + q
                e, k = divmod(q, 2)
                sl = token_slice(b)
                dve.wait_ge(th_ready, v + 1)
                if v >= 2:
                    b2, q2 = divmod(v - 2, UNITS)
                    if on_pool(b2, q2):
                        dve.wait_ge(hid_pool, pool_units(b2, q2) + 1)
                    else:
                        dve.wait_ge(hid_dve, dve_units(b2, q2) + 1)
                nc.vector.scalar_tensor_tensor(out=ga[:, v % 2, sl], in0=th[:, v % 2, sl], scalar=1.0,
                                               in1=gate_ps[v % 2][:, sl], op0=ALU.add,
                                               op1=ALU.mult).then_inc(ga_ready, 1)

            def up_mul(b, q):
                if on_pool(b, q):
                    return
                v = UNITS * b + q
                e, k = divmod(q, 2)
                sl = token_slice(b)
                dve.wait_ge(ga_ready, v + 1)
                if FFNS * b + e >= 2:
                    dve.wait_ge(down_done, FFNS * b + e - 1)
                nc.vector.tensor_tensor(hid[:, (FFNS * b + e) % 2, k, sl], ga[:, v % 2, sl], up_ps[v % 2][:, sl],
                                        ALU.mult).then_inc(hid_dve, 1)

            def wide(v, b):
                return (v[:, tile_slice(b)].rearrange("p (t a) -> p t a", a=1)
                        .to_broadcast([P, len(tiles_of(b)), N_EXPERTS]))

            def every_tile(v, b):
                return v[:].rearrange("p (a e) -> p a e", a=1).to_broadcast([P, len(tiles_of(b)), N_EXPERTS])

            def route(b, k):
                tl = tile_slice(b)
                step = ROUTE_STEPS * b + k
                if k >= 1:
                    dve.wait_ge(routed, step)
                onehot, best, key = (oh1, m1, k1) if k <= 10 else (oh2, m2, k2)
                if k == 0:
                    dve.wait_ge(lg_done, b + 1)
                    if b == 0:
                        dve.wait_ge(ld_bias, 16)
                    ins = nc.vector.tensor_tensor(
                        lg[:, tl], misc_ps[:, 0:TILES * N_EXPERTS].rearrange("p (t e) -> p t e", e=N_EXPERTS)[:, tl],
                        every_tile(bias_sb, b), ALU.add)
                elif k == 1:
                    ins = nc.vector.tensor_reduce(r_max[:, tl], lg[:, tl], AX_X, ALU.max)
                elif k == 2:
                    ins = nc.vector.tensor_tensor(lg[:, tl], lg[:, tl], wide(r_max, b), ALU.subtract)
                elif k == 3:
                    dve.wait_ge(ex_ready, b + 1)
                    ins = nc.vector.tensor_reduce(r_sum[:, tl], ex[:, tl], AX_X, ALU.add)
                elif k == 4:
                    ins = nc.vector.reciprocal(r_inv[:, tl], r_sum[:, tl])
                elif k == 5:
                    ins = nc.vector.tensor_tensor(pr[:, tl], ex[:, tl], wide(r_inv, b), ALU.mult)
                elif k in (6, 12):
                    ins = nc.vector.tensor_reduce(best[:, tl], pr[:, tl], AX_X, ALU.max)
                elif k in (7, 13):
                    ins = nc.vector.tensor_tensor(eq[:, tl], pr[:, tl], wide(best, b), ALU.is_equal)
                elif k in (8, 14):
                    if b == 0:
                        dve.wait_ge(consts_ready, N_EXPERTS + 1)
                    ins = nc.vector.tensor_tensor(eq[:, tl], eq[:, tl], every_tile(rev, b), ALU.mult)
                elif k in (9, 15):
                    ins = nc.vector.tensor_reduce(key[:, tl], eq[:, tl], AX_X, ALU.max)
                elif k in (10, 16):
                    ins = nc.vector.tensor_tensor(onehot[:, tl], every_tile(rev, b), wide(key, b), ALU.is_equal)
                elif k == 11:
                    ins = nc.vector.scalar_tensor_tensor(out=pr[:, tl], in0=oh1[:, tl], scalar=-4.0, in1=pr[:, tl],
                                                         op0=ALU.mult, op1=ALU.add)
                elif k == 17:
                    ins = nc.vector.tensor_tensor(r_dif[:, tl], m2[:, tl], m1[:, tl], ALU.subtract)
                elif k == 18:
                    dve.wait_ge(r_exp_ready, b + 1)
                    ins = nc.vector.tensor_scalar(r_den[:, tl], r_exp[:, tl], 2.0, 2.0, ALU.mult, ALU.add)
                elif k == 19:
                    ins = nc.vector.reciprocal(w1[:, tl], r_den[:, tl])
                elif k == 20:
                    ins = nc.vector.tensor_tensor(w2[:, tl], r_exp[:, tl], w1[:, tl], ALU.mult)
                elif k == 21:
                    ins = nc.vector.tensor_tensor(oh1[:, tl], oh1[:, tl], wide(w1, b), ALU.mult)
                elif k == 22:
                    ins = nc.vector.tensor_tensor(oh2[:, tl], oh2[:, tl], wide(w2, b), ALU.mult)
                else:
                    if b >= 2:
                        dve.wait_ge(ffn_moved, FFNS * (b - 1))
                    ins = nc.vector.tensor_tensor(comb[:, b % 2, tl], oh1[:, tl], oh2[:, tl], ALU.add)
                ins.then_inc(routed, 1)

            def route_at(g, place):
                for b in range(len(BLOCKS)):
                    slots = POST_SLOTS[b]
                    k = (g - D_STATE * (b + 1) - slots[ROUTE]) * ROUTE_PLACES + place - (ROUTE_PLACES - 1)
                    if k >= 3:
                        k = max(k - slots[EXP_GAP], 2)
                        if k == 2:
                            continue
                    if k >= 18:
                        k = max(k - slots[TOP_GAP], 17)
                        if k == 17:
                            continue
                    if 0 <= k < ROUTE_STEPS:
                        route(b, k)

            def low(dst, src, hi):
                return nc.vector.tensor_tensor(dst, src, hi.bitcast(F32), ALU.subtract)

            nc.vector.memset(da[:, :, :, 0:1], 0.0).then_inc(zeros_ready, 1)
            nc.vector.memset(xnt_hi[:, 0:PAD].bitcast(F32), 0.0).then_inc(zeros_ready, 1)
            nc.vector.memset(xnt_lo[:, 0:PAD].bitcast(F32), 0.0).then_inc(zeros_ready, 1)
            for g in range(FIRST_SLOT, LAST_SLOT):
                route_at(g, 0)
                if 0 <= g < STEPS:
                    scan(g)
                for c in range(HALVES):
                    if (b := post_at(g, (POST_Y0, POST_Y1)[c])) is not None:
                        if b >= 1:
                            dve.wait_ge(post_done, b)
                        sl = token_slice(b)
                        dve.wait_ge(acc_turned, HALVES * b + c + 1)
                        nc.vector.scalar_tensor_tensor(out=y[:, c, sl], in0=xc[:, BLOCKS[b][0] % 2, c, sl],
                                                       scalar=d_par[:, c:c + 1], in1=misc_ps[:, sl], op0=ALU.mult,
                                                       op1=ALU.add).then_inc(y_added, 1)
                if (b := post_at(g, POST_X2_LOW)) is not None:
                    sl = token_slice(b)
                    dve.wait_ge(x2t_hi_ready, b + 1)
                    low(x2t_lo[:, b % 2, sl], misc_ps[:, sl], x2t_hi[:, b % 2, sl]).then_inc(x2t_lo_ready, 1)
                route_at(g, 1)
                units = units_at(g - 1)
                for i, (b, q) in enumerate(units):
                    if i >= 2:
                        up_mul(*units[i - 2])
                    gate_mul(b, q)
                route_at(g, 2)
                if 1 <= g <= STEPS:
                    add_states(g - 1, 0)
                for b, q in units[-2:]:
                    up_mul(b, q)
                route_at(g, 3)
                if 1 <= g <= STEPS:
                    add_states(g - 1, 1)
                route_at(g, 4)
                if (c := split_piece(g)) is not None:
                    dve.wait_ge(ffn_w_hi, c + 1)
                    low(pieces(ffn_lo, c), pieces(ffn_raw, c), pieces(ffn_hi, c)).then_inc(ffn_w_ready, 1)

                if g == 1:
                    dve.wait_ge(ld_router, 16)
                    nc.vector.tensor_copy(router_hi[:], router_sb[:]).then_inc(router_split, 1)
                    dve.wait_ge(router_split, 1)
                    low(router_lo[:], router_sb[:], router_hi[:]).then_inc(router_split, 1)
                if (s := pre_at(g, PRE_STATS)) is not None:
                    dve.wait_ge(ld_x[s], 16)
                    stats("a", s, range(TILES), lambda t: x[:, s, t, :])
                    if s == 0:
                        dve.wait_ge(ld_w_in, 16)
                        dve.wait_ge(ld_conv, 16)
                        nc.vector.tensor_tensor(tap_raw, conv_raw, w_in_raw[:, 0:D_INNER]
                                                .rearrange("p (a c) -> p a c", a=1)
                                                .to_broadcast([P, D_CONV, D_INNER]), ALU.mult).then_inc(taps_raw, 1)
                if (s := pre_at(g, PRE_NORM)) is not None and not by_scalar("a", s):
                    normalise("a", s, range(TILES), xn, lambda t: x[:, s, t, :]).then_inc(xn_ready, 1)
                if (s := pre_at(g, PRE_TURN)) is not None:
                    if s == 0:
                        dve.wait_ge(w_in_hi, 2)
                        low(gate_w_lo[:], w_in_raw[:, D_INNER:], gate_w_hi[:]).then_inc(w_in_ready, 1)
                        low(tap_lo[:], tap_raw, tap_hi[:]).then_inc(w_in_ready, 1)
                    dve.wait_ge(xnt_hi_ready, s + 1)
                    low(xnt_lo[:, PAD:], pre_bank(s, "xnt")[:], xnt_hi[:, PAD:]).then_inc(xnt_lo_ready, 1)
                if pre_at(g, PRE_DT1) == 0:
                    dve.wait_ge(a_exp_ready, 1)
                    nc.vector.tensor_scalar(a_neg[:].rearrange("p c n -> p (c n)"), a_exp[:], -1.0, None,
                                            ALU.mult).then_inc(a_ready, 1)
                    for c in range(HALVES):
                        dve.wait_ge(sp_step, c + 1)
                        nc.vector.tensor_scalar(sp_relu[:, c, :], pre_bank(0, f"dt{c}")[:], b_dt[:, c:c + 1], 0.0,
                                                ALU.add, ALU.max).then_inc(dt_read, 1)
                if (s := pre_at(g, PRE_END)) is not None:
                    dve.wait_ge(sp_ready, s + 1)
                    dve.wait_ge(dt_read, HALVES * (s + 1))
                    if s >= 1:
                        dve.wait_ge(da_ready, HALVES * D_STATE * s)
                        dve.wait_ge(u_ready, s)
                    nc.vector.tensor_tensor(dt[:], sp_exp[:], sp_relu[:], ALU.add).then_inc(dt_ready, 1)
                    if s == 0:
                        dve.wait_ge(dt_ready, 1)
                        dve.wait_ge(conv_ready, HALVES)
                        nc.vector.tensor_tensor(u[:], dt[:], xc[:, 0], ALU.mult).then_inc(u_ready, 1)
                        dve.wait_ge(u_ready, 1)
                        dve.wait_ge(b_loaded[0], 16)
                        nc.vector.tensor_tensor(dbx[:, 0], u[:], b_all[:, 0:1, :].to_broadcast([P, HALVES, TOKENS]),
                                                ALU.mult).then_inc(first_dbx, 1)

                if (b := post_at(g, POST_STATS)) is not None:
                    dve.wait_ge(post_done, b + 1)
                    stats("b", b, tiles_of(b), lambda t: misc_ps[:, t * D_MODEL:(t + 1) * D_MODEL])
                if (b := post_at(g, POST_ADD)) is not None:
                    s, tl = BLOCKS[b][0], tile_slice(b)
                    if b >= 1:
                        dve.wait_ge(x2_turned, b)
                    normalise("b", b, tiles_of(b), x2,
                              lambda t: misc_ps[:, t * D_MODEL:(t + 1) * D_MODEL]).then_inc(post_read, 1)
                    dve.wait_ge(post_read, b + 1)
                    nc.vector.tensor_tensor(x[:, s, tl], x[:, s, tl], x2[:, tl], ALU.add).then_inc(x1_ready, 1)
                    dve.wait_ge(x1_ready, b + 1)
                    stats("c", b, tiles_of(b), lambda t: x[:, s, t, :])
                if (b := post_at(g, POST_NORM)) is not None:
                    normalise("c", b, tiles_of(b), x2, lambda t: x[:, BLOCKS[b][0], t, :]).then_inc(x2_ready, 1)
                route_at(g, 5)
                if (b := fin_at(g, FIN_STATS)) is not None:
                    dve.wait_ge(ffn_added, N_EXPERTS * (b + 1))
                    stats("f", b, tiles_of(b), lambda t: ffn_sum[:, b % 2, t, :])
                if (b := fin_at(g, FIN_OUT)) is not None and not by_scalar("f", b):
                    part = ffn_sum[:, b % 2, tile_slice(b)]
                    normalise("f", b, tiles_of(b), ffn_sum[:, b % 2],
                              lambda t: ffn_sum[:, b % 2, t, :]).then_inc(fin_scaled, 1)
                    dve.wait_ge(fin_scaled, b + 1)
                    nc.vector.tensor_tensor(part, part, x[:, BLOCKS[b][0], tile_slice(b)],
                                         ALU.add).then_inc(out_ready, 1)

        @block.gpsimd
        def _(pool):
            def rstd(kind, i, tl):
                pool.wait_ge(stats_ready[kind], i + 1)
                nc.gpsimd.tensor_tensor(rs[kind][:, tl], ve[kind][:, tl], half_neg[:, tl],
                                        ALU.pow).then_inc(rs_ready[kind], 1)
                if by_scalar(kind, i):
                    pool.wait_ge(rs_ready[kind], i + 1)
                    nc.gpsimd.tensor_tensor(shift[kind][:, tl], minus_mean[kind][:, tl], rs[kind][:, tl],
                                            ALU.mult).then_inc(shift_ready[kind], 1)

            def inject(m):
                b, n = divmod(m, D_STATE)
                sl = token_slice(b)
                if n == 0 or m == 1:
                    pool.wait_ge(u_ready, BLOCKS[b][0] + 1)
                if n % B_CHUNK == 0 or m == 1:
                    i = m // B_CHUNK
                    pool.wait_ge(b_loaded[i % 2], 16 * (i // 2 + 1))
                if m >= DA_RING:
                    pool.wait_ge(scanned, m - DA_RING + 1)
                nc.gpsimd.tensor_tensor(dbx[:, m % DA_RING, :, sl], u[:, :, sl],
                                        b_all[:, m % B_RING:m % B_RING + 1, sl]
                                        .to_broadcast([P, HALVES, sl.stop - sl.start]), ALU.mult).then_inc(dbx_ready, 1)

            def add_ffn(b, e):
                tl = tile_slice(b)
                pool.wait_ge(ffn_moved, FFNS * b + e + 1)
                if e >= 2:
                    pool.wait_ge(ffn_added, N_EXPERTS * b + e - 1)
                nc.gpsimd.tensor_tensor(ffn_sum[:, b % 2, tl], ffn_sum[:, b % 2, tl],
                                        ffn_one[:, (N_EXPERTS * b + e - 1) % 2, tl], ALU.add).then_inc(ffn_added, 1)

            def mul_up(b, q):
                v = UNITS * b + q
                e, k = divmod(q, 2)
                sl = token_slice(b)
                pool.wait_ge(ga_ready, v + 1)
                i = pool_units(b, q)
                pool.wait_ge(up_ready, i + 1)
                if FFNS * b + e >= 2:
                    pool.wait_ge(down_done, FFNS * b + e - 1)
                nc.gpsimd.tensor_tensor(hid[:, (FFNS * b + e) % 2, k, sl], ga[:, v % 2, sl], up_cp[:, i % 2, sl],
                                        ALU.mult).then_inc(hid_pool, 1)

            nc.gpsimd.memset(ident[:], 0.0).then_inc(ident_zero, 1)
            nc.gpsimd.memset(half_neg[:], -0.5).then_inc(consts_ready, 1)
            for e in range(N_EXPERTS):
                nc.gpsimd.memset(rev[:, e:e + 1], float(N_EXPERTS - e)).then_inc(consts_ready, 1)
            pool.wait_ge(ident_zero, 1)
            nc.gpsimd.affine_select(out=ident[:], in_=ident[:], compare_op=ALU.not_equal, fill=1.0, base=0,
                                    pattern=[[-1, P]], channel_multiplier=1).then_inc(ident_ready, 1)
            pool.wait_ge(consts_ready, N_EXPERTS + 1)
            for g in range(FIRST_SLOT, LAST_SLOT):
                if 1 <= g + LEAD < STEPS:
                    inject(g + LEAD)
                for b, q in units_at(g - 1):
                    if on_pool(b, q):
                        mul_up(b, q)
                for b, e in downs_at(g - 1):
                    if e >= 1:
                        add_ffn(b, e)

                if (s := pre_at(g, PRE_STATS)) is not None:
                    rstd("a", s, slice(0, TILES))
                if (s := pre_at(g, PRE_END)) is not None and s >= 1:
                    pool.wait_ge(dt_ready, s + 1)
                    pool.wait_ge(conv_ready, HALVES * (s + 1))
                    pool.wait_ge(dbx_ready, D_STATE * s - 1)
                    nc.gpsimd.tensor_tensor(u[:], dt[:], xc[:, s % 2], ALU.mult).then_inc(u_ready, 1)
                for c in range(HALVES):
                    if (b := post_at(g, (POST_Y0, POST_Y1)[c])) is not None:
                        sl = token_slice(b)
                        pool.wait_ge(y_added, HALVES * b + c + 1)
                        pool.wait_ge(gz_ready, HALVES * (BLOCKS[b][0] + 1))
                        nc.gpsimd.tensor_tensor(y[:, c, sl], y[:, c, sl], gz[:, BLOCKS[b][0] % 2, c, sl],
                                                ALU.mult).then_inc(y_ready, 1)
                if (b := post_at(g, POST_STATS)) is not None:
                    rstd("b", b, tile_slice(b))
                if (b := post_at(g, POST_ADD)) is not None:
                    rstd("c", b, tile_slice(b))
                if (b := fin_at(g, FIN_OUT)) is not None and by_scalar("f", b):
                    part = ffn_sum[:, b % 2, tile_slice(b)]
                    pool.wait_ge(fin_scaled, b + 1)
                    nc.gpsimd.tensor_tensor(part, part, x[:, BLOCKS[b][0], tile_slice(b)],
                                         ALU.add).then_inc(out_ready, 1)
                if (b := fin_at(g, FIN_STATS)) is not None:
                    rstd("f", b, tile_slice(b))


def kernel(**inputs):
    import numpy as np
    import concourse.bacc as bacc
    from concourse.bass_utils import run_bass_kernel_spmd

    a = {k.removeprefix("L0_"): np.asarray(v) for k, v in inputs.items()}

    w_x = a["attn_W_x"]

    def channels(v):
        return np.moveaxis(v.reshape(HALVES, P, *v.shape[1:]), 0, 1)

    def with_shared(shared, experts, axes):
        return np.ascontiguousarray(np.concatenate([shared[None], experts]).transpose(axes))

    arrays = {
        "x_in": np.ascontiguousarray(a["attn_x"].reshape(SEQS, TILES, P, D_MODEL).transpose(0, 2, 1, 3)),
        "cols": np.ascontiguousarray(np.concatenate(
            [channels(a["attn_conv_b"]), channels(a["attn_b_dt"]), channels(a["attn_D_param"]),
             channels(a["attn_A_log"]).reshape(P, HALVES * D_STATE)], axis=1)),
        "w_in": np.ascontiguousarray(a["attn_W_in"]),
        "conv_t": np.ascontiguousarray(a["attn_conv_w"].T),
        "w_x": np.ascontiguousarray(channels(np.concatenate(
            [w_x[:, :DT_RANK], w_x[:, DT_RANK + D_STATE:], w_x[:, DT_RANK:DT_RANK + D_STATE]], axis=1))),
        "w_dt": np.ascontiguousarray(a["attn_W_dt"]),
        "w_out": np.ascontiguousarray(channels(a["attn_W_out"])),
        "router_t": np.ascontiguousarray(a["ffn_router_w"].T),
        "bias_r": np.ascontiguousarray(a["ffn_expert_bias"]),
        "gate_t": with_shared(a["ffn_sw_gate"], a["ffn_ew_gate"], (2, 0, 1)),
        "up_t": with_shared(a["ffn_sw_up"], a["ffn_ew_up"], (2, 0, 1)),
        "down_t": np.ascontiguousarray(np.concatenate([a["ffn_sw_down"][None], a["ffn_ew_down"]])
                                       .reshape(FFNS, D_MODEL, 2, P).transpose(3, 0, 2, 1)),
    }
    nc = bacc.Bacc("TRN2", target_bir_lowering=False, num_devices=1)
    args = [nc.dram_tensor(k, v.shape, F32, kind="ExternalInput").ap() for k, v in arrays.items()]
    b_scratch = nc.dram_tensor("b_scratch", (SEQS, D_STATE, TOKENS), F32, kind="Internal").ap()
    out = nc.dram_tensor("out", (SEQS, P, TILES, D_MODEL), F32, kind="ExternalOutput").ap()
    build(nc, *args, b_scratch, out)
    r = run_bass_kernel_spmd(nc, [arrays], core_ids=[0])
    got = np.asarray(r.results[0]["out"])
    return np.ascontiguousarray(got.transpose(0, 2, 1, 3)).reshape(SEQS, TOKENS, D_MODEL)
```
